# Optimizing a Trainium2 kernel written in Bass

```python
import numpy as np
import jax
import jax.numpy as jnp

def _softmax(x, axis=-1):
    return jax.nn.softmax(x, axis=axis)

def _gelu(x):
    return jax.nn.gelu(x, approximate=True)

def _silu(x):
    return jax.nn.silu(x)

def _sigmoid(x):
    return jax.nn.sigmoid(x)

def _layernorm(x, axis=-1, eps=1e-05):
    m = jnp.mean(x, axis=axis, keepdims=True)
    v = jnp.var(x, axis=axis, keepdims=True)
    return (x - m) / jnp.sqrt(v + eps)

def _scatter_add(tgt, idx, src, axis=0):
    return tgt.at[idx].add(src)

def _segment_sum(src, seg, n):
    return jax.ops.segment_sum(src, seg, n)
kernel_name = 'mk_lm_tower_d1_tok_ids1024_r4_5ba6ae'

def setup_inputs(seed: int=0):
    np.random.seed(seed)
    _w = jnp.asarray

    def _rec_inputs():
        import jax
        import jax.numpy as jnp
        _rk = jax.random.key(seed)
        x = jax.random.randint(jax.random.fold_in(_rk, 1), (2, 1024), 0, 2048, jnp.int32)
        return x
    x = _rec_inputs()

    def _L0_tok_setup():
        import jax, jax.numpy as jnp
        import numpy as np
        CODEBOOK_SIZE = 2048
        CODEBOOK_DIM = 256
        HIDDEN_DIM = 1024
        OUT_DIM = 256
        B, M = (32, 144)
        key = jax.random.key(seed)
        k_idx, k_cb, k_w1, k_w2 = jax.random.split(key, 4)
        index = jax.random.randint(k_idx, (B, M), 0, CODEBOOK_SIZE, dtype=jnp.int32)
        codebook = CODEBOOK_DIM ** 0.5 * jax.random.normal(k_cb, (CODEBOOK_SIZE, CODEBOOK_DIM), dtype=jnp.float32)
        s1 = 1.0 / np.sqrt(CODEBOOK_DIM)
        s2 = 1.0 / np.sqrt(HIDDEN_DIM)
        W1 = s1 * jax.random.normal(k_w1, (CODEBOOK_DIM, HIDDEN_DIM), dtype=jnp.float32)
        b1 = jnp.zeros((HIDDEN_DIM,), dtype=jnp.float32)
        W2 = s2 * jax.random.normal(k_w2, (HIDDEN_DIM, OUT_DIM), dtype=jnp.float32)
        b2 = jnp.zeros((OUT_DIM,), dtype=jnp.float32)
        return {'index': index, 'codebook': codebook, 'W1': W1, 'b1': b1, 'W2': W2, 'b2': b2}
    _L0_tok_all = _L0_tok_setup()
    _L0_tok_in = {k: v for k, v in _L0_tok_all.items() if k in ('codebook', 'W1', 'b1', 'W2', 'b2')}
    del _L0_tok_all

    def _L0_attn_setup():
        import jax, jax.numpy as jnp
        import numpy as np
        from jax import lax
        L, B, S, D, H = (2, 8, 512, 256, 256)
        LOG_H0 = float(np.log(0.5))

        def _log_g(x):
            return jnp.where(x >= 0, jnp.log(jnp.where(x >= 0, x + 0.5, 1.0)), -jax.nn.softplus(-x))

        def _mingru_layer(x, Wz, bz, Wh, bh):
            k = jnp.einsum('bsd,hd->bsh', x, Wz) + bz
            log_z = -jax.nn.softplus(-k)
            log_coeffs = -jax.nn.softplus(k)
            pre_h = jnp.einsum('bsd,hd->bsh', x, Wh) + bh
            log_values = log_z + _log_g(pre_h)
            Bq = x.shape[0]
            log_coeffs = jnp.pad(log_coeffs, ((0, 0), (1, 0), (0, 0)))
            log_values = jnp.concatenate([jnp.full((Bq, 1, log_values.shape[-1]), LOG_H0, dtype=log_values.dtype), log_values], axis=1)
            a_star = jnp.cumsum(log_coeffs, axis=1)
            log_h = a_star + lax.cumlogsumexp(log_values - a_star, axis=1)
            return jnp.exp(log_h)[:, 1:]
        key = jax.random.key(seed)
        ks = jax.random.split(key, 5)
        stdv = 1.0 / np.sqrt(D)
        u = lambda k, shp: jax.random.uniform(k, shp, jnp.float32, -stdv, stdv)
        return {'x': jax.random.normal(ks[0], (B, S, D), jnp.float32), 'Wz': u(ks[1], (L, H, D)), 'bz': u(ks[2], (L, H)), 'Wh': u(ks[3], (L, H, D)), 'bh': u(ks[4], (L, H))}
    _L0_attn_all = _L0_attn_setup()
    _L0_attn_in = {k: v for k, v in _L0_attn_all.items() if k in ('Wz', 'bz', 'Wh', 'bh')}
    del _L0_attn_all

    def _L0_ffn_setup():
        import jax, jax.numpy as jnp
        import numpy as np
        HIDDEN = 256
        INTER = 1024
        N_EXPERTS = 8

        def geglu(x, w1, w2, w3):
            return jax.nn.gelu(x @ w1, approximate=False) * (x @ w2) @ w3
        key = jax.random.key(seed)
        ks = jax.random.split(key, 8)
        s = 0.02
        x = jax.random.normal(ks[0], (2, 512, HIDDEN), dtype=jnp.float32)
        w1s = jax.random.normal(ks[1], (HIDDEN, INTER), dtype=jnp.float32) * s
        w2s = jax.random.normal(ks[2], (HIDDEN, INTER), dtype=jnp.float32) * s
        w3s = jax.random.normal(ks[3], (INTER, HIDDEN), dtype=jnp.float32) * s
        W1 = jax.random.normal(ks[4], (N_EXPERTS, HIDDEN, INTER), dtype=jnp.float32) * s
        W2 = jax.random.normal(ks[5], (N_EXPERTS, HIDDEN, INTER), dtype=jnp.float32) * s
        W3 = jax.random.normal(ks[6], (N_EXPERTS, INTER, HIDDEN), dtype=jnp.float32) * s
        Wg = jax.random.normal(ks[7], (HIDDEN, N_EXPERTS), dtype=jnp.float32) * s
        return {'x': x, 'w1s': w1s, 'w2s': w2s, 'w3s': w3s, 'W1': W1, 'W2': W2, 'W3': W3, 'Wg': Wg}
    _L0_ffn_all = _L0_ffn_setup()
    _L0_ffn_in = {k: v for k, v in _L0_ffn_all.items() if k in ('w1s', 'w2s', 'w3s', 'W1', 'W2', 'W3', 'Wg')}
    del _L0_ffn_all
    return {'x': x, 'L0_tok_codebook': _L0_tok_in['codebook'], 'L0_tok_W1': _L0_tok_in['W1'], 'L0_tok_b1': _L0_tok_in['b1'], 'L0_tok_W2': _L0_tok_in['W2'], 'L0_tok_b2': _L0_tok_in['b2'], 'L0_attn_Wz': _L0_attn_in['Wz'], 'L0_attn_bz': _L0_attn_in['bz'], 'L0_attn_Wh': _L0_attn_in['Wh'], 'L0_attn_bh': _L0_attn_in['bh'], 'L0_ffn_w1s': _L0_ffn_in['w1s'], 'L0_ffn_w2s': _L0_ffn_in['w2s'], 'L0_ffn_w3s': _L0_ffn_in['w3s'], 'L0_ffn_W1': _L0_ffn_in['W1'], 'L0_ffn_W2': _L0_ffn_in['W2'], 'L0_ffn_W3': _L0_ffn_in['W3'], 'L0_ffn_Wg': _L0_ffn_in['Wg']}

def reference(x, L0_tok_codebook, L0_tok_W1, L0_tok_b1, L0_tok_W2, L0_tok_b2, L0_attn_Wz, L0_attn_bz, L0_attn_Wh, L0_attn_bh, L0_ffn_w1s, L0_ffn_w2s, L0_ffn_w3s, L0_ffn_W1, L0_ffn_W2, L0_ffn_W3, L0_ffn_Wg):
    import jax
    import jax.numpy as jnp

    def _L0_tok_ref(index, codebook, W1, b1, W2, b2):
        import jax, jax.numpy as jnp
        import numpy as np
        CODEBOOK_SIZE = 2048
        CODEBOOK_DIM = 256
        HIDDEN_DIM = 1024
        OUT_DIM = 256
        B, M = (32, 144)
        quantized = jnp.take(codebook, index, axis=0)
        h = jax.nn.gelu(jnp.einsum('bmd,dh->bmh', quantized, W1) + b1)
        rec = jnp.einsum('bmh,ho->bmo', h, W2) + b2
        return rec

    def _L0_attn_ref(x, Wz, bz, Wh, bh):
        import jax, jax.numpy as jnp
        import numpy as np
        from jax import lax
        L, B, S, D, H = (2, 8, 512, 256, 256)
        LOG_H0 = float(np.log(0.5))

        def _log_g(x):
            return jnp.where(x >= 0, jnp.log(jnp.where(x >= 0, x + 0.5, 1.0)), -jax.nn.softplus(-x))

        def _mingru_layer(x, Wz, bz, Wh, bh):
            k = jnp.einsum('bsd,hd->bsh', x, Wz) + bz
            log_z = -jax.nn.softplus(-k)
            log_coeffs = -jax.nn.softplus(k)
            pre_h = jnp.einsum('bsd,hd->bsh', x, Wh) + bh
            log_values = log_z + _log_g(pre_h)
            Bq = x.shape[0]
            log_coeffs = jnp.pad(log_coeffs, ((0, 0), (1, 0), (0, 0)))
            log_values = jnp.concatenate([jnp.full((Bq, 1, log_values.shape[-1]), LOG_H0, dtype=log_values.dtype), log_values], axis=1)
            a_star = jnp.cumsum(log_coeffs, axis=1)
            log_h = a_star + lax.cumlogsumexp(log_values - a_star, axis=1)
            return jnp.exp(log_h)[:, 1:]
        h = x
        for l in range(Wz.shape[0]):
            h = _mingru_layer(h, Wz[l], bz[l], Wh[l], bh[l])
        return h

    def _L0_ffn_ref(x, w1s, w2s, w3s, W1, W2, W3, Wg):
        import jax, jax.numpy as jnp
        import numpy as np
        HIDDEN = 256
        INTER = 1024
        N_EXPERTS = 8

        def geglu(x, w1, w2, w3):
            return jax.nn.gelu(x @ w1, approximate=False) * (x @ w2) @ w3
        B, T, C = x.shape
        xf = x.reshape(-1, C)
        shared = geglu(xf, w1s, w2s, w3s)
        logits = xf @ Wg
        idx = jnp.argmax(logits, axis=-1)
        final = jnp.zeros_like(xf)
        for e in range(N_EXPERTS):
            y = geglu(xf, W1[e], W2[e], W3[e])
            final = final + jnp.where((idx == e)[:, None], y, 0.0)
        return (shared + final).reshape(B, T, C)
    h = _L0_tok_ref(x, L0_tok_codebook, L0_tok_W1, L0_tok_b1, L0_tok_W2, L0_tok_b2)
    h = h + _L0_attn_ref(_layernorm(h, axis=-1), L0_attn_Wz, L0_attn_bz, L0_attn_Wh, L0_attn_bh)
    h = h + _L0_ffn_ref(_layernorm(h, axis=-1), L0_ffn_w1s, L0_ffn_w2s, L0_ffn_w3s, L0_ffn_W1, L0_ffn_W2, L0_ffn_W3, L0_ffn_Wg)
    return h

_drawn_inputs = setup_inputs


def setup_inputs(seed=0):
    import zlib

    import numpy as np

    out = dict(_drawn_inputs(seed))
    spreads = {'L0_tok_b1': (0.0, 0.8), 'L0_tok_b2': (0.0, 0.8)}
    factors = {'L0_attn_Wz': 8.0,
     'L0_attn_bz': 21.489,
     'L0_attn_bh': 8.0,
     'L0_ffn_w1s': 8.0,
     'L0_ffn_w2s': 8.0,
     'L0_ffn_w3s': 8.0,
     'L0_ffn_W1': 8.0,
     'L0_ffn_W2': 8.0,
     'L0_ffn_W3': 8.0,
     'L0_ffn_Wg': 8.0}
    for name, (base, spread) in spreads.items():
        noise = np.random.default_rng([zlib.crc32(name.encode()), seed]).standard_normal(out[name].shape)
        drawn = base * np.exp(spread * noise) if base else spread * noise
        out[name] = jnp.asarray(drawn.astype(out[name].dtype))
    for name, factor in factors.items():
        out[name] = (out[name] * factor).astype(out[name].dtype)
    return out
```

```python
from contextlib import ExitStack

import concourse.bass as bass
from concourse import mybir

P = 128
ALU = mybir.AluOpType
ACT = mybir.ActivationFunctionType
AX = mybir.AxisListType.X
F32 = mybir.dt.float32
F32R = mybir.dt.float32r
I32 = mybir.dt.int32
U16 = mybir.dt.uint16
EPS = 1e-5
H0 = 0.5


def build(nc, idx, codebook, tok_w1, tok_b1, tok_w2, tok_b2, gru_wz, gru_bz, gru_wh, gru_bh,
          w1s, w2s, w3s, ew1, ew2, ew3, wg, out):
    TILES = idx.shape[1]
    D = codebook.shape[1]
    KD = D // P
    HID = tok_w1.shape[2]
    HC = HID // P
    NB = 512
    BT = NB // P
    BLOCKS = TILES // BT
    LAYERS = gru_wz.shape[1]
    BATCH = 2
    SB = BLOCKS // BATCH
    EXPERTS = ew1.shape[0]
    XT = TILES + EXPERTS - 1
    LT = TILES + XT
    NH = HID // NB
    WCH = KD * HID
    PART = 3 * WCH
    SLOT = 2 * PART
    GW = LAYERS * KD * D

    x_sorted = nc.dram_tensor("x_sorted", [XT * P, D], F32, kind="Internal").ap()
    y_sorted = nc.dram_tensor("y_sorted", [XT * P, D], F32, kind="Internal").ap()

    with ExitStack() as ctx:
        place = [17 * 1024]

        def at(name, shape, dt, offset):
            return nc.alloc_sbuf_tensor_at(name, shape, dt, offset=offset)

        def region(kib):
            here = place[0]
            place[0] += kib * 1024
            return here

        def small(name, shape, dt=F32):
            size = 4
            for n in shape[1:]:
                size *= n
            here = place[0]
            place[0] += -(-size // 32) * 32
            return at(name, shape, dt, here)

        def sem(name):
            return ctx.enter_context(nc.semaphore(name))

        r_slots = region(96)
        r_stage = region(24)
        r_x1hi = region(16)
        r_x1lo = region(16)
        r_gruw = region(16)
        r_res = region(16)
        K = 1024

        w_slots = at("w_slots", [P, 2 * SLOT], F32R, r_slots)
        w1p = at("w1p", [P, 2, KD, HID], F32R, r_slots)
        w2p = at("w2p", [P, 2, HC, D], F32R, r_slots + 16 * K)
        hTp = at("hTp", [P, 2, HC, NB], F32R, r_slots + 32 * K)
        qTp = at("qTp", [P, 2, KD, NB], F32R, r_slots + 64 * K)
        q = at("q", [P, BT, D], F32, r_slots + 72 * K)
        xnb = at("xnb", [P, BT, D], F32, r_slots + 76 * K)
        h0p = at("h0p", [P, 2, KD, TILES * P], F32R, r_slots + 48 * K)
        RG = 3
        HF = 2
        a_gate = at("a_gate", [P, RG, NB], F32, r_slots + 80 * K)
        v_gate = at("v_gate", [P, RG, NB], F32, r_slots + 86 * K)
        h_full = at("h_full", [P, HF, NB], F32, r_slots + 92 * K)
        fetched = at("fetched", [P, TILES, D], F32, r_slots)

        stage = at("stage", [P, 3, WCH], F32, r_stage)
        x1hi = at("x1hi", [P, KD, TILES * P], F32R, r_x1hi)
        x1lo = at("x1lo", [P, KD, TILES * P], F32R, r_x1lo)
        h1 = at("h1", [P, KD, TILES * P], F32, r_x1hi)
        xlT = at("xlT", [P, TILES, KD, P], F32, r_x1hi)
        xn2 = at("xn2", [P, TILES, D], F32, r_x1lo)
        gruw = at("gruw", [P, 2, 2, LAYERS, KD, D], F32R, r_gruw)
        g_buf = at("g_buf", [P, HID], F32, r_gruw)
        gelu_buf = at("gelu_buf", [P, NH, NB], F32, r_gruw + 4 * K)
        gTp = at("gTp", [P, 2, HC, P], F32R, r_gruw + 8 * K)
        res = at("res", [P, TILES, D], F32, r_res)

        ident = small("ident", [P, P])
        before = small("before", [P, P])
        ones = small("ones", [P, P])
        b2r = small("b2r", [P, D])
        x_row = small("x_row", [P, D])
        xTp = small("xTp", [P, 2, KD, P], F32R)
        y_row = small("y_row", [P, D])
        zero_row = small("zero_row", [P, D])
        idx_sb = small("idx_sb", [P, TILES], I32)
        b1 = small("b1", [P, HC])
        bz = small("bz", [P, LAYERS * KD])
        bh = small("bh", [P, LAYERS * KD])
        nbz = small("nbz", [P, LAYERS * KD])
        bh5 = small("bh5", [P, LAYERS * KD])
        wgs = small("wgs", [P, KD, EXPERTS])
        stats = small("stats", [P, BT, 6])
        mv = small("mv", [P, 2 * BT, 2])
        veps = small("veps", [P, BT])
        rstd = small("rstd", [P, 2 * TILES])
        mhalf = small("mhalf", [P, BT])
        carry = small("carry", [P, BATCH * KD])

        TE = TILES * EXPERTS
        logits = small("logits", [P, TILES, EXPERTS])
        best = small("best", [P, TILES])
        rank8 = small("rank8", [P, TILES, EXPERTS])
        score = small("score", [P, TILES, EXPERTS])
        first = small("first", [P, TILES])
        onehot = small("onehot", [P, TILES, EXPERTS])
        ranks = small("ranks", [P, 2, TE])
        totals = small("totals", [P, EXPERTS, TILES])
        upto = small("upto", [P, TE])
        counts = small("counts", [P, EXPERTS])
        steps = small("steps", [P, EXPERTS, TILES])
        over = small("over", [P, EXPERTS, TILES])
        tiles_e = small("tiles_e", [P, EXPERTS])
        tiles_upto = small("tiles_upto", [P, EXPERTS])
        first_row = small("first_row", [P, EXPERTS])
        shift = small("shift", [P, EXPERTS])
        base = small("base", [P, EXPERTS, TILES])
        place_te = small("place_te", [P, TILES, EXPERTS])
        pos_f = small("pos_f", [P, TILES])
        pos = small("pos", [P, TILES], I32)
        tile_no = small("tile_no", [P, XT, EXPERTS - 1])
        past = small("past", [P, XT, EXPERTS - 1])
        sign = small("sign", [P, XT, EXPERTS - 1])
        past_s = small("past_s", [P, XT, EXPERTS - 1])
        expert_f = small("expert_f", [P, XT])
        odd_f = small("odd_f", [P, XT])
        need_w = small("need_w", [P, LT], U16)
        slot_at = small("slot_at", [P, LT], U16)
        slot_next = small("slot_next", [P, LT], U16)
        splits_at = small("splits_at", [P, LT], U16)
        fresh = small("fresh", [P, XT])
        more = small("more", [P, XT])

        up_banks = (0, 1, 2, 7)
        rec_banks = (3, 6)
        flip_banks = (4, 5)
        late_banks = (6, 7)
        ps = ctx.enter_context(nc.psum_tensor("ps", [P, 8, NB], F32))

        idx_land = sem("idx_land"); small_land = sem("small_land"); b_land = sem("b_land")
        stage_land = [sem(f"stage_land{c}") for c in range(3)]
        expert_land = [sem(f"expert_land{c}") for c in range(3)]
        q_land = [sem(f"q_land{b}") for b in range(BLOCKS)]
        zeroed = sem("zeroed"); zero_set = sem("zero_set")
        pool_const = sem("pool_const"); dve_const = sem("dve_const")
        w1_hi = sem("w1_hi"); w1_lo = sem("w1_lo"); w2_hi = sem("w2_hi"); w2_lo = sem("w2_lo"); gru_hi = sem("gru_hi"); gru_lo = sem("gru_lo")
        qT_ps = sem("qT_ps"); qT_hi = sem("qT_hi"); qT_lo = sem("qT_lo")
        h_ps = sem("h_ps"); h_gelu = sem("h_gelu"); h_hi = sem("h_hi"); h_lo = sem("h_lo")
        rec_ps = sem("rec_ps"); rec_done = sem("rec_done"); bn_done = sem("bn_done"); mv_done = sem("mv_done")
        veps_done = sem("veps_done"); rstd_done = sem("rstd_done"); xn_done = sem("xn_done")
        xT_ps = sem("xT_ps"); x1_hi = sem("x1_hi"); x1_lo = sem("x1_lo")
        k_ps = sem("k_ps"); p_ps = sem("p_ps"); gates = sem("gates"); gate_steps = sem("gate_steps")
        scanned = sem("scanned"); carried = sem("carried"); h0_hi = sem("h0_hi"); h0_lo = sem("h0_lo")
        h1T_ps = sem("h1T_ps"); res_done = sem("res_done"); bn2_done = sem("bn2_done"); mv2_done = sem("mv2_done")
        xn2_done = sem("xn2_done"); xl_ps = sem("xl_ps"); xl_act = sem("xl_act"); xl_dve = sem("xl_dve")
        logit_ps = sem("logit_ps"); onehot_done = sem("onehot_done"); rank_ps = sem("rank_ps"); onehot_steps = sem("onehot_steps")
        router = sem("router"); routed = sem("routed"); scattered = sem("scattered")
        x_land = sem("x_land"); x_ps = sem("x_ps"); xT_hi = sem("xT_hi"); xT_lo = sem("xT_lo")
        a_ps = sem("a_ps"); b_ps = sem("b_ps"); gelu_done = sem("gelu_done"); g_done = sem("g_done")
        gT_ps = sem("gT_ps"); gT_hi = sem("gT_hi"); gT_lo = sem("gT_lo")
        tile_done = sem("tile_done"); y_taken = sem("y_taken"); y_stored = sem("y_stored")
        split_hi = sem("split_hi"); pool_turn = sem("pool_turn"); act_turn = sem("act_turn"); placed = sem("placed"); split_lo = sem("split_lo")
        fetch_land = [sem(f"fetch_land{b}") for b in range(BLOCKS)]
        summed = sem("summed"); out_stored = sem("out_stored")

        def f32(ap):
            return ap.bitcast(F32)

        def mm3(pe, dst, lhs_hi, lhs_lo, rhs_hi, rhs_lo, start, stop):
            pe.matmul(dst, lhs_hi, rhs_hi, start=start, stop=False)
            pe.matmul(dst, lhs_hi, rhs_lo, start=False, stop=False)
            return pe.matmul(dst, lhs_lo, rhs_hi, start=False, stop=stop)

        block_order = [c * SB + s for s in range(SB) for c in range(BATCH)]
        units = [(layer, b, hc) for layer in range(LAYERS) for b in block_order for hc in range(KD)]
        U0 = len(units) // LAYERS
        last_unit = {(layer, b): u for u, (layer, b, hc) in enumerate(units)}

        FLIP_AFTER = HC // 2 + 1

        block = ctx.enter_context(nc.Block())

        @block.sync
        def _(sp):
            sp.dma_start(idx_sb[:], idx).then_inc(idx_land, 16)
            sp.dma_start(stage[:, 0, :], tok_w1.rearrange("p k n -> p (k n)")).then_inc(stage_land[0], 16)
            sp.dma_start(b1[:], tok_b1).then_inc(small_land, 16)
            sp.dma_start(bz[:], gru_bz).then_inc(small_land, 16)
            sp.dma_start(bh[:], gru_bh).then_inc(small_land, 16)
            sp.dma_start(wgs[:], wg).then_inc(small_land, 16)
            sp.dma_start(b2r[:], tok_b2.to_broadcast([P, D])).then_inc(small_land, 16)
            sp.dma_start(stage[:, 1, :], tok_w2.rearrange("p k n -> p (k n)")).then_inc(stage_land[1], 16)
            sp.dma_start(stage[:, 2, 0:GW], gru_wz.rearrange("p l k n -> p (l k n)")).then_inc(stage_land[2], 16)
            sp.dma_start(stage[:, 2, GW:2 * GW], gru_wh.rearrange("p l k n -> p (l k n)")).then_inc(stage_land[2], 16)
            sp.wait_ge(zero_set, 1)
            sp.wait_ge(qT_ps, 1)
            with sp.Fori(0, XT) as j:
                sp.dma_start(x_sorted[bass.ds(j * P, P), :], zero_row[:]).then_inc(zeroed, 16)
            sp.wait_ge(w1_lo, 2)
            sp.dma_start(stage[:, 0, :], w1s).then_inc(stage_land[0], 16)
            sp.wait_ge(w2_lo, 1)
            sp.dma_start(stage[:, 1, :], w2s).then_inc(stage_land[1], 16)
            sp.wait_ge(gru_lo, 1)
            sp.dma_start(stage[:, 2, :], w3s).then_inc(stage_land[2], 16)

            sp.wait_ge(xn2_done, TILES)
            sp.dma_start(x_row[:], xn2[:, 0, :]).then_inc(x_land, 16)
            with sp.Fori(1, TILES) as i:
                sp.wait_ge(x_ps, i)
                sp.dma_start(x_row[:], xn2[:, bass.ds(i, 1), :].rearrange("p a d -> p (a d)")).then_inc(x_land, 16)
            sp.wait_ge(scattered, 16 * TILES)
            sp.wait_ge(x_ps, TILES)
            sp.dma_start(x_row[:], x_sorted[0:P, :]).then_inc(x_land, 16)
            sp.wait_ge(x_ps, TILES + 1)
            sp.dma_start(x_row[:], x_sorted[P:2 * P, :]).then_inc(x_land, 16)
            with sp.Fori(2, XT) as j:
                sp.wait_ge(x_ps, j + TILES)
                sp.dma_start(x_row[:], x_sorted[bass.ds(j * P, P), :]).then_inc(x_land, 16)
                sp.wait_ge(y_taken, j + (TILES - 1))
                sp.dma_start(y_sorted[bass.ds(j * P - 2 * P, P), :], y_row[:]).then_inc(y_stored, 16)
            for j in (XT - 2, XT - 1):
                sp.wait_ge(y_taken, TILES + j + 1)
                sp.dma_start(y_sorted[j * P:(j + 1) * P, :], y_row[:]).then_inc(y_stored, 16)

            out_v = out.rearrange("(b i p) d -> b p i d", i=BT, p=P)
            for b in range(BLOCKS):
                sp.wait_ge(summed, b + 1)
                sp.dma_start(out_v[b], fetched[:, b * BT:(b + 1) * BT, :]).then_inc(out_stored, 16)
            sp.wait_ge(out_stored, 16 * BLOCKS)

        @block.gpsimd
        def _(pool):
            pool.memset(ident[:], 0.0).then_inc(pool_const, 1)
            pool.wait_ge(pool_const, 1)
            pool.affine_select(out=ident[:], in_=ident[:], compare_op=ALU.not_equal, fill=1.0, base=0,
                               pattern=[[-1, P]], channel_multiplier=1).then_inc(pool_const, 1)

            def gather(b):
                for i in range(BT):
                    pool.indirect_dma_start(
                        out=q[:, i, :], out_offset=None, in_=codebook,
                        in_offset=bass.IndirectOffsetOnAxis(ap=idx_sb[:, b * BT + i:b * BT + i + 1], axis=0),
                        bounds_check=codebook.shape[0] - 1, oob_is_err=True).then_inc(q_land[b], 16)

            pool.wait_ge(idx_land, 16)
            gather(0)
            pool.memset(zero_row[:], 0.0).then_inc(zero_set, 1)
            pool.memset(mhalf[:], -0.5).then_inc(pool_const, 1)

            pool.wait_ge(qT_ps, 2)
            gather(1)
            pool.memset(before[:], 1.0).then_inc(pool_const, 1)
            pool.wait_ge(pool_const, 4)
            pool.affine_select(out=before[:], in_=before[:], compare_op=ALU.is_gt, fill=0.0, base=0,
                               pattern=[[1, P]], channel_multiplier=-1).then_inc(pool_const, 1)
            pool.iota(rank8[:], [[0, TILES], [-1, EXPERTS]], base=EXPERTS, channel_multiplier=0,
                      allow_small_or_imprecise_dtypes=True).then_inc(pool_const, 1)
            pool.iota(steps[:], [[0, EXPERTS], [P, TILES]], base=0, channel_multiplier=0,
                      allow_small_or_imprecise_dtypes=True).then_inc(pool_const, 1)
            pool.iota(tile_no[:], [[1, XT], [0, EXPERTS - 1]], base=0, channel_multiplier=0,
                      allow_small_or_imprecise_dtypes=True).then_inc(pool_const, 1)

            norms = [0]

            def rstd_of(done, need, half):
                n = norms[0]
                norms[0] += 1
                pool.wait_ge(done, need)
                if n == 0:
                    pool.wait_ge(pool_const, 3)
                else:
                    pool.wait_ge(rstd_done, n)
                pool.tensor_scalar(veps[:], mv[:, half * BT:(half + 1) * BT, 1], EPS, None, ALU.add).then_inc(veps_done, 1)
                pool.wait_ge(veps_done, n + 1)
                pool.tensor_tensor(rstd[:, n * BT:(n + 1) * BT], veps[:], mhalf[:], ALU.pow).then_inc(rstd_done, 1)

            for b in range(BLOCKS):
                if b + 2 < BLOCKS:
                    pool.wait_ge(qT_ps, 2 * (b + 2))
                    gather(b + 2)
                rstd_of(mv_done, (b + 1) * BT, b % 2)

            def split(s, slot):
                for c in range(3):
                    o = slot * SLOT + c * WCH
                    hi = w_slots[:, o:o + WCH]
                    if s == 0:
                        pool.wait_ge(stage_land[c], 32 if c < 2 else 48)
                    else:
                        pool.wait_ge(expert_land[c], 16 * s)
                    pool.tensor_scalar(hi, stage[:, c, :], 1.0, 1.0, ALU.mult, ALU.mult).then_inc(split_hi, 1)
                    pool.wait_ge(split_hi, s * 3 + c + 1)
                    pool.tensor_tensor(w_slots[:, o + PART:o + PART + WCH], stage[:, c, :], f32(hi),
                                       ALU.subtract).then_inc(split_lo, 1)
                    pool.wait_ge(split_lo, s * 3 + c + 1)
                    load(s, c)

            def load(e, c):
                src = (ew1, ew2, ew3)[c]
                if isinstance(e, int):
                    pool.dma_start(stage[:, c, :], src[e]).then_inc(expert_land[c], 16)
                else:
                    pool.dma_start(stage[:, c, :], src[bass.ds(e, 1)].rearrange("a p n -> p (a n)")).then_inc(expert_land[c], 16)

            split(0, 0)
            for n, b in enumerate(block_order):
                rstd_of(mv2_done, (n + 1) * BT, n % 2)
            pool.wait_ge(xl_ps, TILES // 2)
            split(1, 1)

            pool.wait_ge(placed, 1)
            pool.wait_ge(zeroed, 16 * XT)
            for t in range(TILES):
                pool.indirect_dma_start(
                    out=x_sorted, out_offset=bass.IndirectOffsetOnAxis(ap=pos[:, t:t + 1], axis=0),
                    in_=xn2[:, t, :], in_offset=None,
                    bounds_check=XT * P - 1, oob_is_err=True).then_inc(scattered, 16)

            with pool.Fori(2, EXPERTS) as e:
                for c in range(3):
                    pool.wait_ge(split_lo, e * 3 + (c + 1))
                    pool.sem_inc(pool_turn, 1)
                    load(e, c)

            pool.wait_ge(y_stored, 16 * XT)
            for t in range(TILES):
                pool.indirect_dma_start(
                    out=fetched[:, t, :], out_offset=None, in_=y_sorted,
                    in_offset=bass.IndirectOffsetOnAxis(ap=pos[:, t:t + 1], axis=0),
                    bounds_check=XT * P - 1, oob_is_err=True).then_inc(fetch_land[t // BT], 16)

        @block.tensor
        def _(pe):
            def q_transposes(b):
                pe.wait_ge(q_land[b], 16 * BT)
                if b == 0:
                    pe.wait_ge(pool_const, 2)
                elif b == 1:
                    pe.wait_ge(qT_lo, 2)
                else:
                    pe.wait_ge(x1_lo, 2 * (b - 1))
                for k in range(KD):
                    for i in range(BT):
                        last = pe.transpose(ps[:, flip_banks[k], i * P:(i + 1) * P], q[:, i, k * P:(k + 1) * P], ident[:])
                    last.then_inc(qT_ps, 1)

            def mlp_up(b):
                pe.wait_ge(qT_lo, 2 * (b + 1))
                for h in range(HC):
                    n = b * HC + h
                    if n == 0:
                        pe.wait_ge(w1_lo, 1)
                    if n == HC // 2:
                        pe.wait_ge(w1_lo, 2)
                    if n >= len(up_banks):
                        pe.wait_ge(h_lo, n - len(up_banks) + 1)
                    for k in range(KD):
                        cols = slice(h * P, (h + 1) * P)
                        last = mm3(pe, ps[:, up_banks[n % len(up_banks)], :], w1p[:, 0, k, cols], w1p[:, 1, k, cols],
                                   qTp[:, 0, k, :], qTp[:, 1, k, :], k == 0, k == KD - 1)
                    last.then_inc(h_ps, 1)
                    if b and h == FLIP_AFTER:
                        x_transposes(b - 1, flip_banks)

            def x_transposes(b, banks):
                pe.wait_ge(xn_done, BT * (b + 1))
                if banks == flip_banks:
                    pe.wait_ge(qT_lo, 2 * (b + 2))
                else:
                    pe.wait_ge(rec_done, TILES)
                for k in range(KD):
                    for i in range(BT):
                        last = pe.transpose(ps[:, banks[k], i * P:(i + 1) * P], xnb[:, i, k * P:(k + 1) * P], ident[:])
                    last.then_inc(xT_ps, 1)

            def mlp_down(b):
                pe.wait_ge(h_lo, HC * (b + 1))
                if b == 0:
                    pe.wait_ge(w2_lo, 1)
                for i in range(BT):
                    t = b * BT + i
                    if t >= 2:
                        pe.wait_ge(rec_done, t - 1)
                    for h in range(HC):
                        cols = slice(i * P, (i + 1) * P)
                        last = mm3(pe, ps[:, rec_banks[t % 2], 0:D], hTp[:, 0, h, cols], hTp[:, 1, h, cols],
                                   w2p[:, 0, h, :], w2p[:, 1, h, :], h == 0, h == HC - 1)
                    last.then_inc(rec_ps, 1)

            q_transposes(0)
            for b in range(BLOCKS):
                mlp_up(b)
                if b + 1 < BLOCKS:
                    q_transposes(b + 1)
                mlp_down(b)

            def gru(u):
                layer, b, hc = units[u]
                cols = slice(b * NB, (b + 1) * NB)
                if layer == 0:
                    src = lambda part, k: (x1hi, x1lo)[part][:, k, cols]
                    pe.wait_ge(x1_lo, 2 * (b + 1))
                else:
                    src = lambda part, k: h0p[:, part, k, cols]
                    pe.wait_ge(h0_lo, last_unit[0, b] + 1)
                if u == 0:
                    pe.wait_ge(gru_lo, 1)
                if u == 1:
                    pe.wait_ge(rec_done, TILES)
                if u >= RG:
                    pe.wait_ge(scanned, u - RG + 1)
                for g, done in enumerate((k_ps, p_ps)):
                    for k in range(KD):
                        w = slice(hc * P, (hc + 1) * P)
                        last = mm3(pe, ps[:, 2 * (u % RG) + g, :], gruw[:, 0, g, layer, k, w], gruw[:, 1, g, layer, k, w],
                                   src(0, k), src(1, k), k == 0, k == KD - 1)
                    last.then_inc(done, 1)

            def state_transposes(n):
                b = block_order[n]
                pe.wait_ge(scanned, last_unit[1, b] + 1)
                if n == 0:
                    pe.wait_ge(x1_lo, 2 * BLOCKS)
                for i in range(BT):
                    if n:
                        pe.wait_ge(res_done, (n - 1) * BT + i // 2 * 2 + 2)
                    for k in range(KD):
                        t = b * BT + i
                        last = pe.transpose(ps[:, 6 + i // 2, (i % 2) * D + k * P:(i % 2) * D + (k + 1) * P],
                                            h1[:, k, t * P:(t + 1) * P], ident[:])
                    if i % 2:
                        last.then_inc(h1T_ps, 1)

            for u in range(len(units)):
                gru(u)
                if u == KD - 1:
                    x_transposes(BLOCKS - 1, late_banks)
                n = (u - U0) // KD - 1
                if u >= U0 and (u - U0) % KD == KD - 1 and n >= 0:
                    state_transposes(n)
            state_transposes(BLOCKS - 1)

            for b in range(BLOCKS):
                for i in range(BT):
                    n = b * BT + i
                    t = block_order[b] * BT + i
                    pe.wait_ge(xn2_done, n + 1)
                    if n == BT * (BLOCKS - 1):
                        pe.wait_ge(res_done, TILES)
                    for k in range(KD):
                        at_ = (n % 2) * D + k * P
                        last = pe.transpose(ps[:, n // 2, at_:at_ + P], xn2[:, t, k * P:(k + 1) * P], ident[:])
                    if n % 2:
                        last.then_inc(xl_ps, 1)
            pe.wait_ge(small_land, 80)
            pe.wait_ge(xl_act, TILES // 4)
            pe.wait_ge(xl_dve, TILES // 4)
            for t in range(TILES):
                for k in range(KD):
                    last = pe.matmul(ps[:, 7, t * EXPERTS:(t + 1) * EXPERTS], xlT[:, t, k, :], wgs[:, k, :],
                                     start=(k == 0), stop=(k == KD - 1))
            last.then_inc(logit_ps, 1)

            def up(i, slot):
                pe.wait_ge(xT_lo, i + 1)
                for n in range(NH):
                    for w, (bank, done) in enumerate(((0, a_ps), (2, b_ps))):
                        for k in range(KD):
                            o = w * WCH + k * HID + n * NB
                            last = mm3(pe, ps[:, bank + n, :], xTp[:, 0, k, :], xTp[:, 1, k, :],
                                       w_slots[:, bass.ds(slot + o, NB)], w_slots[:, bass.ds(slot + (o + PART), NB)],
                                       k == 0, k == KD - 1)
                        last.then_inc(done, 1)

            def row_transposes(i):
                pe.wait_ge(x_land, 16 * (i + 1))
                for k in range(KD):
                    last = pe.transpose(ps[:, 6, k * P:(k + 1) * P], x_row[:, k * P:(k + 1) * P], ident[:])
                last.then_inc(x_ps, 1)

            def down(i, slot):
                pe.wait_ge(gT_lo, 2 * (i + 1))
                for c in range(HC):
                    o = 2 * WCH + c * D
                    last = mm3(pe, ps[:, 7, 0:D], gTp[:, 0, c, :], gTp[:, 1, c, :],
                               w_slots[:, bass.ds(slot + o, D)], w_slots[:, bass.ds(slot + (o + PART), D)],
                               c == 0, c == HC - 1)
                last.then_inc(tile_done, 1)

            def g_transposes(i):
                for n in range(NH):
                    pe.wait_ge(g_done, 2 * i + n + 1)
                    for c in range(HC // NH):
                        j = n * (HC // NH) + c
                        last = pe.transpose(ps[:, 4 + n, c * P:(c + 1) * P], g_buf[:, j * P:(j + 1) * P], ident[:])
                    last.then_inc(gT_ps, 1)

            pe.wait_ge(split_lo, 3)
            row_transposes(0)
            up(0, 0)
            row_transposes(1)
            pe.wait_ge(onehot_done, 1)
            pe.wait_ge(pool_const, 8)
            pe.wait_ge(dve_const, 1)
            oh = onehot[:].rearrange("p t e -> p (t e)")
            pe.matmul(ps[:, 7, 0:TE], before[:], oh, start=True, stop=True)
            pe.matmul(ps[:, 7, TE:2 * TE], ones[:], oh, start=True, stop=True).then_inc(rank_ps, 1)
            g_transposes(0)
            pe.wait_ge(router, 1)
            up(1, 0)
            row_transposes(2)
            down(0, 0)
            g_transposes(1)
            with pe.Fori(2, TILES) as i:
                up(i, 0)
                row_transposes(i + 1)
                pe.wait_ge(y_taken, i - 1)
                down(i - 1, 0)
                g_transposes(i)
            pe.wait_ge(routed, 1)

            def slot_of(i):
                return pe.value_load(slot_at[0:1, bass.ds(i, 1)], min_val=0, max_val=SLOT)

            def routed_tile(i, last):
                splits = pe.value_load(need_w[0:1, bass.ds(i, 1)], min_val=0, max_val=3 * (EXPERTS + 1))
                here, before_ = slot_of(i), slot_of(i - 1)
                pe.wait_ge(split_lo, splits)
                up(i, here)
                if not last:
                    row_transposes(i + 1)
                pe.wait_ge(y_taken, i - 1)
                down(i - 1, before_)
                g_transposes(i)

            with pe.Fori(TILES, LT - 1) as i:
                routed_tile(i, False)
            routed_tile(LT - 1, True)
            here = slot_of(LT - 1)
            pe.wait_ge(y_taken, LT - 1)
            down(LT - 1, here)

        @block.scalar
        def _(act):
            w1v = stage[:, 0, :].rearrange("p (k n) -> p k n", k=KD)
            act.preload_act_table(ACT.Gelu_apprx_tanh)
            act.wait_ge(stage_land[0], 16)
            for h in range(2):
                cols = slice(h * NB, (h + 1) * NB)
                act.activation(w1p[:, 0, :, cols], w1v[:, :, cols], ACT.Copy).then_inc(w1_hi, 1)
            act.wait_ge(stage_land[1], 16)
            act.activation(w2p[:, 0].rearrange("p k n -> p (k n)"), stage[:, 1, :], ACT.Copy).then_inc(w2_hi, 1)

            def q_hi(b):
                for k in range(KD):
                    act.wait_ge(qT_ps, 2 * b + k + 1)
                    act.activation(qTp[:, 0, k, :], ps[:, flip_banks[k], :], ACT.Copy).then_inc(qT_hi, 1)

            def x_hi(b, banks):
                for k in range(KD):
                    act.wait_ge(xT_ps, 2 * b + k + 1)
                    act.activation(x1hi[:, k, b * NB:(b + 1) * NB], ps[:, banks[k], :], ACT.Copy).then_inc(x1_hi, 1)

            q_hi(0)
            act.wait_ge(stage_land[2], 32)
            act.activation(gruw[:, 0].rearrange("p g l k n -> p (g l k n)"), stage[:, 2, :], ACT.Copy).then_inc(gru_hi, 1)
            act.wait_ge(small_land, 80)
            for b in range(BLOCKS):
                for h in range(HC):
                    n = b * HC + h
                    act.wait_ge(h_ps, n + 1)
                    act.activation(ps[:, up_banks[n % len(up_banks)], :], ps[:, up_banks[n % len(up_banks)], :], ACT.Gelu_apprx_tanh,
                                   bias=b1[:, h:h + 1]).then_inc(h_gelu, 1)
                    act.wait_ge(h_gelu, n + 1)
                    act.activation(hTp[:, 0, h, :], ps[:, up_banks[n % len(up_banks)], :], ACT.Copy).then_inc(h_hi, 1)
                    if b and h == FLIP_AFTER:
                        x_hi(b - 1, flip_banks)
                if b + 1 < BLOCKS:
                    q_hi(b + 1)

            def state_hi(u):
                _, b, hc = units[u]
                act.wait_ge(scanned, u + 1)
                act.activation(h0p[:, 0, hc, b * NB:(b + 1) * NB], h_full[:, u % HF, :], ACT.Copy).then_inc(h0_hi, 1)

            act.preload_act_table(ACT.Sigmoid)
            act.wait_ge(dve_const, 1)
            for u, (layer, b, hc) in enumerate(units):
                c = layer * KD + hc
                bank = 2 * (u % RG)
                act.wait_ge(k_ps, u + 1)
                act.activation(a_gate[:, u % RG, :], ps[:, bank, :], ACT.Sigmoid, bias=nbz[:, c:c + 1],
                               scale=-1.0).then_inc(gates, 1)
                act.activation(ps[:, bank, :], ps[:, bank, :], ACT.Sigmoid, bias=bz[:, c:c + 1]).then_inc(gates, 1)
                act.wait_ge(p_ps, u + 1)
                act.activation(v_gate[:, u % RG, :], ps[:, bank + 1, :], ACT.Sigmoid,
                               bias=bh[:, c:c + 1]).then_inc(gates, 1)
                if 1 <= u <= U0:
                    state_hi(u - 1)
                if u == KD - 1:
                    x_hi(BLOCKS - 1, late_banks)

            act.preload_act_table(ACT.Gelu)
            for m in range(0, TILES // 2, 2):
                t = block_order[2 * m // BT] * BT + 2 * m % BT
                act.wait_ge(xl_ps, m + 1)
                act.activation(xlT[:, t:t + 2, :, :].rearrange("p t k n -> p (t k n)"), ps[:, m, :], ACT.Copy).then_inc(xl_act, 1)

            def row_hi(i):
                act.wait_ge(x_ps, i + 1)
                act.activation(xTp[:, 0, :, :].rearrange("p k n -> p (k n)"), ps[:, 6, 0:D], ACT.Copy).then_inc(xT_hi, 1)

            def tile(i, last=False):
                for n in range(NH):
                    act.wait_ge(a_ps, 2 * i + n + 1)
                    act.activation(gelu_buf[:, n, :], ps[:, n, :], ACT.Gelu).then_inc(gelu_done, 1)
                if not last:
                    row_hi(i + 1)
                for n in range(NH):
                    act.wait_ge(gT_ps, 2 * i + n + 1)
                    act.activation(gTp[:, 0, n * BT:(n + 1) * BT, :].rearrange("p c n -> p (c n)"), ps[:, 4 + n, :],
                                   ACT.Copy).then_inc(gT_hi, 1)

            row_hi(0)
            with act.Fori(0, TILES) as i:
                tile(i)

            def next_hi(i):
                first = act.value_load(splits_at[0:1, bass.ds(i, 1)], min_val=0, max_val=EXPERTS)
                with act.If(first > 0):
                    s = act.value_load(splits_at[0:1, bass.ds(i, 1)], min_val=1, max_val=EXPERTS)
                    to = act.value_load(slot_next[0:1, bass.ds(i, 1)], min_val=0, max_val=SLOT)
                    for c in range(3):
                        act.wait_ge(expert_land[c], s * 16)
                        act.sem_inc(act_turn, 1)
                        act.activation(w_slots[:, bass.ds(to + c * WCH, WCH)], stage[:, c, :], ACT.Copy).then_inc(split_hi, 1)

            act.wait_ge(routed, 1)
            with act.Fori(TILES, LT - 1) as i:
                tile(i)
                next_hi(i)
            tile(LT - 1, last=True)

        @block.vector
        def _(dve):
            w1v = stage[:, 0, :].rearrange("p (k n) -> p k n", k=KD)
            for h in range(2):
                cols = slice(h * NB, (h + 1) * NB)
                dve.wait_ge(w1_hi, h + 1)
                dve.tensor_tensor(w1p[:, 1, :, cols], w1v[:, :, cols], f32(w1p[:, 0, :, cols]), ALU.subtract).then_inc(w1_lo, 1)

            def q_lo(b):
                for k in range(KD):
                    dve.wait_ge(qT_hi, 2 * b + k + 1)
                    dve.tensor_tensor(qTp[:, 1, k, :], ps[:, flip_banks[k], :], f32(qTp[:, 0, k, :]), ALU.subtract).then_inc(qT_lo, 1)

            def x_lo(b, banks):
                for k in range(KD):
                    cols = slice(b * NB, (b + 1) * NB)
                    dve.wait_ge(x1_hi, 2 * b + k + 1)
                    dve.tensor_tensor(x1lo[:, k, cols], ps[:, banks[k], :], f32(x1hi[:, k, cols]), ALU.subtract).then_inc(x1_lo, 1)

            def moments(source, n, half, waited, bn, mvs):
                i = n % BT
                dve.wait_ge(waited, n + 1)
                dve.bn_stats(stats[:, i, :], source).then_inc(bn, 1)
                dve.wait_ge(bn, n + 1)
                dve.bn_aggr(mv[:, half * BT + i, :], stats[:, i, :]).then_inc(mvs, 1)

            def normed(dst, source, n, half, i, done):
                m = half * BT + i
                return dve.tensor_scalar(dst, source, mv[:, m, 0:1], rstd[:, n * BT + i:n * BT + i + 1],
                                         ALU.subtract, ALU.mult).then_inc(done, 1)

            def x_norm(b, i):
                if i == 0:
                    dve.wait_ge(rstd_done, b + 1)
                    if b:
                        dve.wait_ge(xT_ps, 2 * b)
                normed(xnb[:, i, :], res[:, b * BT + i, :], b, b % 2, i, xn_done)

            dve.wait_ge(w2_hi, 1)
            dve.tensor_tensor(w2p[:, 1].rearrange("p k n -> p (k n)"), stage[:, 1, :],
                              f32(w2p[:, 0].rearrange("p k n -> p (k n)")), ALU.subtract).then_inc(w2_lo, 1)
            q_lo(0)
            dve.wait_ge(gru_hi, 1)
            dve.tensor_tensor(gruw[:, 1].rearrange("p g l k n -> p (g l k n)"), stage[:, 2, :],
                              f32(gruw[:, 0].rearrange("p g l k n -> p (g l k n)")), ALU.subtract).then_inc(gru_lo, 1)
            dve.wait_ge(small_land, 80)
            for b in range(BLOCKS):
                for h in range(HC):
                    n = b * HC + h
                    if b and h < BT:
                        x_norm(b - 1, h)
                    dve.wait_ge(h_hi, n + 1)
                    dve.tensor_tensor(hTp[:, 1, h, :], ps[:, up_banks[n % len(up_banks)], :], f32(hTp[:, 0, h, :]), ALU.subtract).then_inc(h_lo, 1)
                    if b and h == FLIP_AFTER:
                        x_lo(b - 1, flip_banks)
                if b + 1 < BLOCKS:
                    q_lo(b + 1)
                if b == 0:
                    dve.memset(ones[:], 1.0)
                    dve.memset(sign[:], 1.0)
                    dve.tensor_scalar(nbz[:], bz[:], -1.0, None, ALU.mult)
                    dve.tensor_scalar(bh5[:], bh[:], 0.5, None, ALU.add).then_inc(dve_const, 1)
                for i in range(BT):
                    t = b * BT + i
                    dve.wait_ge(rec_ps, t + 1)
                    dve.tensor_tensor(res[:, t, :], ps[:, rec_banks[t % 2], 0:D], b2r[:], ALU.add).then_inc(rec_done, 1)
                    moments(res[:, t, :], t, b % 2, rec_done, bn_done, mv_done)

            for i in range(BT):
                x_norm(BLOCKS - 1, i)

            def residual(n):
                for i in range(BT):
                    t = block_order[n] * BT + i
                    m = n * BT + i
                    dve.wait_ge(h1T_ps, m // 2 + 1)
                    dve.tensor_tensor(res[:, t, :], ps[:, 6 + i // 2, (i % 2) * D:(i % 2 + 1) * D], res[:, t, :],
                                      ALU.add).then_inc(res_done, 1)
                    moments(res[:, t, :], m, n % 2, res_done, bn2_done, mv2_done)

            def x2_norm(n):
                dve.wait_ge(rstd_done, BLOCKS + n + 1)
                for i in range(BT):
                    t = block_order[n] * BT + i
                    normed(xn2[:, t, :], res[:, t, :], BLOCKS + n, n % 2, i, xn2_done)

            def state_lo(u):
                _, b, hc = units[u]
                cols = slice(b * NB, (b + 1) * NB)
                dve.wait_ge(h0_hi, u + 1)
                dve.tensor_tensor(h0p[:, 1, hc, cols], h_full[:, u % HF, :], f32(h0p[:, 0, hc, cols]),
                                  ALU.subtract).then_inc(h0_lo, 1)

            carries = 0
            dve.wait_ge(dve_const, 1)
            for u, (layer, b, hc) in enumerate(units):
                c = layer * KD + hc
                bank = 2 * (u % RG)
                g = v_gate[:, u % RG, :]
                dve.wait_ge(gates, 3 * u + 3)
                dve.scalar_tensor_tensor(out=g, in0=ps[:, bank + 1, :], scalar=bh5[:, c:c + 1], in1=g, op0=ALU.add,
                                         op1=ALU.max).then_inc(gate_steps, 1)
                dve.wait_ge(gate_steps, 2 * u + 1)
                dve.tensor_tensor(g, ps[:, bank, :], g, ALU.mult).then_inc(gate_steps, 1)
                if u == KD - 1:
                    x_lo(BLOCKS - 1, late_banks)
                dve.wait_ge(gate_steps, 2 * u + 2)
                first_block = b % SB == 0
                if layer == 0:
                    if u >= HF:
                        dve.wait_ge(h0_lo, u - HF + 1)
                    h = h_full[:, u % HF, :]
                    m = (b // SB) * KD + hc
                    init = H0 if first_block else carry[:, m:m + 1]
                    if not first_block:
                        dve.wait_ge(carried, carries)
                else:
                    h = h1[:, hc, b * NB:(b + 1) * NB]
                    init = H0 if first_block else h1[:, hc, b * NB - 1:b * NB]
                    if not first_block:
                        dve.wait_ge(scanned, last_unit[1, b - 1] + 1)
                dve.tensor_tensor_scan(h, a_gate[:, u % RG, :], g, init, ALU.mult, ALU.add).then_inc(scanned, 1)
                if layer == 0 and first_block:
                    dve.wait_ge(scanned, u + 1)
                    dve.tensor_copy(carry[:, m:m + 1], h[:, NB - 1:NB]).then_inc(carried, 1)
                    carries += 1
                if 1 <= u <= U0:
                    state_lo(u - 1)
                n = (u - U0) // KD - 1
                if u >= U0 and (u - U0) % KD == KD - 1 and n >= 0:
                    residual(n)
                    if n:
                        x2_norm(n - 1)
            residual(BLOCKS - 1)
            x2_norm(BLOCKS - 2)
            x2_norm(BLOCKS - 1)

            for m in range(1, TILES // 2, 2):
                t = block_order[2 * m // BT] * BT + 2 * m % BT
                dve.wait_ge(xl_ps, m + 1)
                dve.tensor_copy(xlT[:, t:t + 2, :, :].rearrange("p t k n -> p (t k n)"), ps[:, m, :]).then_inc(xl_dve, 1)

            steps_done = [0]

            def step(ins):
                steps_done[0] += 1
                ins.then_inc(router, 1)
                dve.wait_ge(router, steps_done[0])

            def over_experts(ap):
                return ap.unsqueeze(2).to_broadcast([P, TILES, EXPERTS])

            dve.wait_ge(logit_ps, 1)
            dve.wait_ge(pool_const, 8)
            chosen = [0]

            def choose(ins):
                chosen[0] += 1
                ins.then_inc(onehot_steps, 1)
                dve.wait_ge(onehot_steps, chosen[0])

            choose(dve.tensor_copy(logits[:].rearrange("p t e -> p (t e)"), ps[:, 7, 0:TE]))
            choose(dve.tensor_reduce(best[:], logits[:], AX, ALU.max))
            choose(dve.tensor_tensor(score[:], logits[:], over_experts(best[:]), ALU.is_ge))
            choose(dve.tensor_tensor(score[:], score[:], rank8[:], ALU.mult))
            choose(dve.tensor_reduce(first[:], score[:], AX, ALU.max))
            dve.tensor_tensor(onehot[:], rank8[:], over_experts(first[:]), ALU.is_equal).then_inc(onehot_done, 1)

            def row_lo(i):
                dve.wait_ge(xT_hi, i + 1)
                dve.tensor_tensor(xTp[:, 1, :, :].rearrange("p k n -> p (k n)"), ps[:, 6, 0:D],
                                  f32(xTp[:, 0, :, :].rearrange("p k n -> p (k n)")), ALU.subtract).then_inc(xT_lo, 1)

            def gated(i):
                for n in range(NH):
                    dve.wait_ge(gelu_done, 2 * i + n + 1)
                    dve.wait_ge(b_ps, 2 * i + n + 1)
                    dve.tensor_tensor(g_buf[:, n * NB:(n + 1) * NB], ps[:, 2 + n, :], gelu_buf[:, n, :],
                                      ALU.mult).then_inc(g_done, 1)

            def gated_lo(i):
                for n in range(NH):
                    half = slice(n * BT, (n + 1) * BT)
                    dve.wait_ge(gT_hi, 2 * i + n + 1)
                    dve.tensor_tensor(gTp[:, 1, half, :].rearrange("p c n -> p (c n)"), ps[:, 4 + n, :],
                                      f32(gTp[:, 0, half, :].rearrange("p c n -> p (c n)")), ALU.subtract).then_inc(gT_lo, 1)

            def add_shared(i):
                r = res[:, bass.ds(i, 1), :].rearrange("p a d -> p (a d)")
                dve.wait_ge(tile_done, i + 1)
                dve.tensor_tensor(r, ps[:, 7, 0:D], r, ALU.add).then_inc(y_taken, 1)

            def take_routed(i):
                dve.wait_ge(tile_done, i + 1)
                return dve.tensor_copy(y_row[:], ps[:, 7, 0:D]).then_inc(y_taken, 1)

            row_lo(0)
            gated(0)
            row_lo(1)
            dve.wait_ge(rank_ps, 1)
            dve.tensor_copy(ranks[:].rearrange("p a n -> p (a n)"), ps[:, 7, 0:2 * TE]).then_inc(router, 1)
            steps_done[0] = 1
            gated_lo(0)

            dve.wait_ge(router, 1)
            step(dve.tensor_copy(totals[:], ranks[:, 1, :].rearrange("p (t e) -> p e t", e=EXPERTS)))
            flat = totals[:].rearrange("p e t -> p (e t)")
            step(dve.tensor_tensor_scan(upto[:], ones[:, 0:TE], flat, 0.0, ALU.mult, ALU.add))
            step(dve.tensor_tensor(upto[:], upto[:], flat, ALU.subtract))
            step(dve.tensor_reduce(counts[:], totals[:], AX, ALU.add))
            step(dve.memset(steps[:, :, 0:1], -1.0))
            step(dve.tensor_tensor(over[:], counts[:].unsqueeze(2).to_broadcast([P, EXPERTS, TILES]), steps[:], ALU.is_gt))
            step(dve.tensor_reduce(tiles_e[:], over[:], AX, ALU.add))
            step(dve.tensor_tensor_scan(tiles_upto[:], ones[:, 0:EXPERTS], tiles_e[:], 0.0, ALU.mult, ALU.add))
            step(dve.tensor_tensor(first_row[:], tiles_upto[:], tiles_e[:], ALU.subtract))
            upto_v = upto[:].rearrange("p (e t) -> p e t", e=EXPERTS)
            step(dve.scalar_tensor_tensor(out=shift[:], in0=first_row[:], scalar=float(P), in1=upto_v[:, :, 0],
                                          op0=ALU.mult, op1=ALU.subtract))
            step(dve.tensor_tensor(base[:], upto_v, shift[:].unsqueeze(2).to_broadcast([P, EXPERTS, TILES]), ALU.add))
            step(dve.tensor_tensor(place_te[:], ranks[:, 0, :].rearrange("p (t e) -> p t e", e=EXPERTS),
                                   base[:].rearrange("p e t -> p t e"), ALU.add))
            step(dve.tensor_tensor(place_te[:], place_te[:], onehot[:], ALU.mult))
            step(dve.tensor_reduce(pos_f[:], place_te[:], AX, ALU.add))
            dve.tensor_copy(pos[:], pos_f[:]).then_inc(placed, 1)
            upto_b = tiles_upto[:, 0:EXPERTS - 1].unsqueeze(1).to_broadcast([P, XT, EXPERTS - 1])
            step(dve.tensor_tensor(past[:], tile_no[:], upto_b, ALU.is_ge))
            step(dve.memset(sign[:, :, 1::2], -1.0))
            step(dve.tensor_tensor(past_s[:], past[:], sign[:], ALU.mult))
            step(dve.tensor_reduce(expert_f[:], past[:], AX, ALU.add))
            step(dve.tensor_reduce(odd_f[:], past_s[:], AX, ALU.add))
            step(dve.memset(need_w[:, 0:TILES], 3))
            step(dve.memset(slot_at[:, 0:TILES], 0))
            step(dve.tensor_scalar(need_w[:, TILES:LT], expert_f[:], 3.0, 6.0, ALU.mult, ALU.add))
            step(dve.tensor_scalar(slot_at[:, TILES:LT], odd_f[:], -float(SLOT), float(SLOT), ALU.mult, ALU.add))
            step(dve.tensor_scalar(slot_next[:, TILES:LT], odd_f[:], float(SLOT), None, ALU.mult))
            step(dve.memset(fresh[:, 0:1], 1.0))
            step(dve.tensor_tensor(fresh[:, 1:XT], expert_f[:, 1:XT], expert_f[:, 0:XT - 1], ALU.subtract))
            step(dve.tensor_scalar(more[:], expert_f[:], float(EXPERTS - 1), None, ALU.is_lt))
            step(dve.tensor_tensor(fresh[:], fresh[:], more[:], ALU.mult))
            step(dve.tensor_scalar(more[:], expert_f[:], 2.0, None, ALU.add))
            step(dve.tensor_tensor(splits_at[:, TILES:LT], more[:], fresh[:], ALU.mult))
            dve.memset(stats[:, 0, 0:1], 0.0).then_inc(routed, 1)

            def next_lo(i):
                first = dve.value_load(splits_at[0:1, bass.ds(i, 1)], min_val=0, max_val=EXPERTS)
                with dve.If(first > 0):
                    s = dve.value_load(splits_at[0:1, bass.ds(i, 1)], min_val=1, max_val=EXPERTS)
                    to = dve.value_load(slot_next[0:1, bass.ds(i, 1)], min_val=0, max_val=SLOT)
                    for c in range(3):
                        dve.wait_ge(split_hi, s * 3 + (c + 1))
                        dve.tensor_tensor(w_slots[:, bass.ds(to + (PART + c * WCH), WCH)], stage[:, c, :],
                                          f32(w_slots[:, bass.ds(to + c * WCH, WCH)]), ALU.subtract).then_inc(split_lo, 1)

            with dve.Fori(1, TILES) as i:
                gated(i)
                row_lo(i + 1)
                add_shared(i - 1)
                gated_lo(i)
            gated(TILES)
            row_lo(TILES + 1)
            add_shared(TILES - 1)
            gated_lo(TILES)
            dve.wait_ge(routed, 1)
            next_lo(TILES)
            gated(TILES + 1)
            row_lo(TILES + 2)
            take_routed(TILES)
            gated_lo(TILES + 1)
            next_lo(TILES + 1)
            with dve.Fori(TILES + 2, LT - 1) as i:
                gated(i)
                row_lo(i + 1)
                dve.wait_ge(y_stored, 16 * i - 16 * (TILES + 1))
                take_routed(i - 1)
                gated_lo(i)
                next_lo(i)
            gated(LT - 1)
            dve.wait_ge(y_stored, 16 * (XT - 2))
            take_routed(LT - 2)
            gated_lo(LT - 1)
            dve.wait_ge(y_stored, 16 * (XT - 1))
            take_routed(LT - 1)

            dve.wait_ge(y_taken, TILES)
            for b in range(BLOCKS):
                v = slice(b * BT, (b + 1) * BT)
                dve.wait_ge(fetch_land[b], 16 * BT)
                dve.tensor_tensor(fetched[:, v, :], fetched[:, v, :], res[:, v, :], ALU.add).then_inc(summed, 1)


def kernel(x, L0_tok_codebook, L0_tok_W1, L0_tok_b1, L0_tok_W2, L0_tok_b2, L0_attn_Wz, L0_attn_bz, L0_attn_Wh,
           L0_attn_bh, L0_ffn_w1s, L0_ffn_w2s, L0_ffn_w3s, L0_ffn_W1, L0_ffn_W2, L0_ffn_W3, L0_ffn_Wg):
    import numpy as np
    import concourse.bacc as bacc
    from concourse import mybir as mb
    from concourse.bass_utils import run_bass_kernel_spmd

    def rows(a):
        a = np.asarray(a)
        k, n = a.shape[-2:]
        a = a.reshape(*a.shape[:-2], k // P, P, n)
        return np.swapaxes(a, -3, -2)

    def flat(a):
        a = rows(a)
        return a.reshape(*a.shape[:-2], -1)

    def column(a):
        return np.asarray(a).reshape(-1, P).T

    def gru(a):
        return rows(np.swapaxes(np.asarray(a), 1, 2)).transpose(1, 0, 2, 3)

    x = np.asarray(x)
    data = {
        "idx": x.reshape(-1, P).T,
        "codebook": np.asarray(L0_tok_codebook),
        "tok_w1": rows(L0_tok_W1), "tok_b1": column(L0_tok_b1),
        "tok_w2": rows(L0_tok_W2), "tok_b2": np.asarray(L0_tok_b2).reshape(1, -1),
        "gru_wz": gru(L0_attn_Wz), "gru_bz": column(L0_attn_bz),
        "gru_wh": gru(L0_attn_Wh), "gru_bh": column(L0_attn_bh),
        "w1s": flat(L0_ffn_w1s), "w2s": flat(L0_ffn_w2s), "w3s": flat(L0_ffn_w3s),
        "ew1": flat(L0_ffn_W1), "ew2": flat(L0_ffn_W2), "ew3": flat(L0_ffn_W3),
        "wg": rows(L0_ffn_Wg),
    }
    nc = bacc.Bacc("TRN2", target_bir_lowering=False, num_devices=1)
    arrays, args = {}, {}
    for name, a in data.items():
        a = np.ascontiguousarray(a)
        arrays[name + "_in"] = a
        args[name] = nc.dram_tensor(name + "_in", a.shape, mb.dt.from_np(a.dtype), kind="ExternalInput").ap()
    d = data["codebook"].shape[1]
    args["out"] = nc.dram_tensor("out_rows", (x.size, d), mb.dt.float32, kind="ExternalOutput").ap()
    build(nc, **args)
    r = run_bass_kernel_spmd(nc, [arrays], core_ids=[0])
    return r.results[0]["out_rows"].reshape(*x.shape, d)
```

```python
from contextlib import ExitStack

import concourse.bass as bass
from concourse import mybir

P = 128
ALU = mybir.AluOpType
ACT = mybir.ActivationFunctionType
AX = mybir.AxisListType.X
F32 = mybir.dt.float32
F32R = mybir.dt.float32r
I32 = mybir.dt.int32
U16 = mybir.dt.uint16
EPS = 1e-5
H0 = 0.5


def build(nc, idx, codebook, tok_w1, tok_b1, tok_w2, tok_b2, gru_wz, gru_bz, gru_wh, gru_bh,
          w1s, w2s, w3s, ew1, ew2, ew3, wg, out):
    TILES = idx.shape[1]
    D = codebook.shape[1]
    KD = D // P
    HID = tok_w1.shape[2]
    HC = HID // P
    NB = 512
    BT = NB // P
    BLOCKS = TILES // BT
    LAYERS = gru_wz.shape[1]
    BATCH = 2
    SB = BLOCKS // BATCH
    EXPERTS = ew1.shape[0]
    XT = TILES + EXPERTS - 1
    LT = TILES + XT
    FRONT = TILES // 2
    BACK = TILES - FRONT
    B0 = FRONT + XT
    SPLITS = EXPERTS + 2
    NH = HID // NB
    WCH = KD * HID
    PART = 3 * WCH
    SLOT = 2 * PART
    GW = LAYERS * KD * D

    x_sorted = nc.dram_tensor("x_sorted", [XT * P, D], F32, kind="Internal").ap()
    y_sorted = nc.dram_tensor("y_sorted", [XT * P, D], F32, kind="Internal").ap()

    with ExitStack() as ctx:
        place = [17 * 1024]

        def at(name, shape, dt, offset):
            return nc.alloc_sbuf_tensor_at(name, shape, dt, offset=offset)

        def region(kib):
            here = place[0]
            place[0] += kib * 1024
            return here

        def small(name, shape, dt=F32):
            size = 4
            for n in shape[1:]:
                size *= n
            here = place[0]
            place[0] += -(-size // 32) * 32
            return at(name, shape, dt, here)

        def sem(name):
            return ctx.enter_context(nc.semaphore(name))

        r_slots = region(96)
        r_stage = region(24)
        r_x1hi = region(16)
        r_x1lo = region(16)
        r_gruw = region(16)
        r_res = region(16)
        K = 1024

        w_slots = at("w_slots", [P, 2 * SLOT], F32R, r_slots)
        w1p = at("w1p", [P, 2, KD, HID], F32R, r_slots)
        w2p = at("w2p", [P, 2, HC, D], F32R, r_slots + 16 * K)
        hTp = at("hTp", [P, 2, HC, NB], F32R, r_slots + 32 * K)
        qTp = at("qTp", [P, 2, KD, NB], F32R, r_slots + 64 * K)
        q = at("q", [P, BT, D], F32, r_slots + 72 * K)
        xnb = at("xnb", [P, BT, D], F32, r_slots + 76 * K)
        h0p = at("h0p", [P, 2, KD, TILES * P], F32R, r_slots + 48 * K)
        RG = 3
        HF = 2
        a_gate = at("a_gate", [P, RG, NB], F32, r_slots + 80 * K)
        v_gate = at("v_gate", [P, RG, NB], F32, r_slots + 86 * K)
        h_full = at("h_full", [P, HF, NB], F32, r_slots + 92 * K)
        fetched = at("fetched", [P, TILES, D], F32, r_stage)

        stage = at("stage", [P, 3, WCH], F32, r_stage)
        x1hi = at("x1hi", [P, KD, TILES * P], F32R, r_x1hi)
        x1lo = at("x1lo", [P, KD, TILES * P], F32R, r_x1lo)
        h1 = at("h1", [P, KD, TILES * P], F32, r_x1hi)
        xlT = at("xlT", [P, TILES, KD, P], F32, r_x1hi)
        xn2 = at("xn2", [P, TILES, D], F32, r_x1lo)
        gruw = at("gruw", [P, 2, 2, LAYERS, KD, D], F32R, r_gruw)
        g_buf = at("g_buf", [P, HID], F32, r_gruw)
        gelu_buf = at("gelu_buf", [P, NH, NB], F32, r_gruw + 4 * K)
        gTp = at("gTp", [P, 2, HC, P], F32R, r_gruw + 8 * K)
        res = at("res", [P, TILES, D], F32, r_res)

        ident = small("ident", [P, P])
        before = small("before", [P, P])
        ones = small("ones", [P, P])
        b2r = small("b2r", [P, D])
        x_row = small("x_row", [P, D])
        xTp = small("xTp", [P, 2, KD, P], F32R)
        y_row = small("y_row", [P, D])
        zero_row = small("zero_row", [P, D])
        idx_sb = small("idx_sb", [P, TILES], I32)
        b1 = small("b1", [P, HC])
        bz = small("bz", [P, LAYERS * KD])
        bh = small("bh", [P, LAYERS * KD])
        nbz = small("nbz", [P, LAYERS * KD])
        bh5 = small("bh5", [P, LAYERS * KD])
        wgs = small("wgs", [P, KD, EXPERTS])
        stats = small("stats", [P, BT, 6])
        mv = small("mv", [P, 2 * BT, 2])
        veps = small("veps", [P, BT])
        rstd = small("rstd", [P, 2 * TILES])
        mhalf = small("mhalf", [P, BT])
        carry = small("carry", [P, BATCH * KD])

        TE = TILES * EXPERTS
        logits = small("logits", [P, TILES, EXPERTS])
        best = small("best", [P, TILES])
        rank8 = small("rank8", [P, TILES, EXPERTS])
        score = small("score", [P, TILES, EXPERTS])
        first = small("first", [P, TILES])
        onehot = small("onehot", [P, TILES, EXPERTS])
        ranks = small("ranks", [P, 2, TE])
        totals = small("totals", [P, EXPERTS, TILES])
        upto = small("upto", [P, TE])
        counts = small("counts", [P, EXPERTS])
        steps = small("steps", [P, EXPERTS, TILES])
        over = small("over", [P, EXPERTS, TILES])
        tiles_e = small("tiles_e", [P, EXPERTS])
        tiles_upto = small("tiles_upto", [P, EXPERTS])
        first_row = small("first_row", [P, EXPERTS])
        shift = small("shift", [P, EXPERTS])
        base = small("base", [P, EXPERTS, TILES])
        place_te = small("place_te", [P, TILES, EXPERTS])
        pos_f = small("pos_f", [P, TILES])
        pos = small("pos", [P, TILES], I32)
        tile_no = small("tile_no", [P, XT, EXPERTS - 1])
        past = small("past", [P, XT, EXPERTS - 1])
        expert_f = small("expert_f", [P, XT])
        turns = small("turns", [P, B0], U16)
        fresh = small("fresh", [P, XT])

        up_banks = (0, 1, 2, 7)
        rec_banks = (3, 6)
        flip_banks = (4, 5)
        late_banks = (6, 7)
        ps = ctx.enter_context(nc.psum_tensor("ps", [P, 8, NB], F32))

        idx_land = sem("idx_land"); small_land = sem("small_land"); b_land = sem("b_land")
        stage_land = [sem(f"stage_land{c}") for c in range(3)]
        expert_land = [sem(f"expert_land{c}") for c in range(3)]
        q_land = [sem(f"q_land{b}") for b in range(BLOCKS)]
        zeroed = sem("zeroed"); zero_set = sem("zero_set")
        pool_const = sem("pool_const"); dve_const = sem("dve_const")
        w1_hi = sem("w1_hi"); w1_lo = sem("w1_lo"); w2_hi = sem("w2_hi"); w2_lo = sem("w2_lo"); gru_hi = sem("gru_hi"); gru_lo = sem("gru_lo")
        qT_ps = sem("qT_ps"); qT_hi = sem("qT_hi"); qT_lo = sem("qT_lo")
        h_ps = sem("h_ps"); h_gelu = sem("h_gelu"); h_hi = sem("h_hi"); h_lo = sem("h_lo")
        rec_ps = sem("rec_ps"); rec_done = sem("rec_done"); bn_done = sem("bn_done"); mv_done = sem("mv_done")
        veps_done = sem("veps_done"); rstd_done = sem("rstd_done"); xn_done = sem("xn_done")
        xT_ps = sem("xT_ps"); x1_hi = sem("x1_hi"); x1_lo = sem("x1_lo")
        k_ps = sem("k_ps"); p_ps = sem("p_ps"); gates = sem("gates"); gate_steps = sem("gate_steps")
        scanned = sem("scanned"); carried = sem("carried"); h0_hi = sem("h0_hi"); h0_lo = sem("h0_lo")
        h1T_ps = sem("h1T_ps"); res_done = sem("res_done"); bn2_done = sem("bn2_done"); mv2_done = sem("mv2_done")
        xn2_done = sem("xn2_done"); xl_ps = sem("xl_ps"); xl_act = sem("xl_act"); xl_dve = sem("xl_dve")
        logit_ps = sem("logit_ps"); onehot_done = sem("onehot_done"); rank_ps = sem("rank_ps"); onehot_steps = sem("onehot_steps")
        router = sem("router"); routed = sem("routed"); scattered = sem("scattered")
        x_land = sem("x_land"); x_ps = sem("x_ps"); xT_hi = sem("xT_hi"); xT_lo = sem("xT_lo")
        a_ps = sem("a_ps"); b_ps = sem("b_ps"); gelu_done = sem("gelu_done"); g_done = sem("g_done")
        gT_ps = sem("gT_ps"); gT_hi = sem("gT_hi"); gT_lo = sem("gT_lo")
        tile_done = sem("tile_done"); y_taken = sem("y_taken"); y_stored = sem("y_stored")
        split_hi = sem("split_hi"); pool_turn = sem("pool_turn"); act_turn = sem("act_turn"); placed = sem("placed"); split_lo = sem("split_lo")
        fetch_land = sem("fetch_land")
        summed = sem("summed"); out_stored = sem("out_stored")

        def f32(ap):
            return ap.bitcast(F32)

        def mm3(pe, dst, lhs_hi, lhs_lo, rhs_hi, rhs_lo, start, stop):
            pe.matmul(dst, lhs_hi, rhs_hi, start=start, stop=False)
            pe.matmul(dst, lhs_hi, rhs_lo, start=False, stop=False)
            return pe.matmul(dst, lhs_lo, rhs_hi, start=False, stop=stop)

        block_order = [c * SB + s for s in range(SB) for c in range(BATCH)]
        units = [(layer, b, hc) for layer in range(LAYERS) for b in block_order for hc in range(KD)]
        U0 = len(units) // LAYERS
        last_unit = {(layer, b): u for u, (layer, b, hc) in enumerate(units)}

        finishes = [slice(0, FRONT // 2), slice(FRONT // 2, FRONT), slice(FRONT, TILES - 3), slice(TILES - 3, TILES - 2),
                    slice(TILES - 2, TILES - 1), slice(TILES - 1, TILES)]

        FLIP_AFTER = HC // 2 + 1

        block = ctx.enter_context(nc.Block())

        @block.sync
        def _(sp):
            sp.dma_start(idx_sb[:], idx).then_inc(idx_land, 16)
            sp.dma_start(stage[:, 0, :], tok_w1.rearrange("p k n -> p (k n)")).then_inc(stage_land[0], 16)
            sp.dma_start(b1[:], tok_b1).then_inc(small_land, 16)
            sp.dma_start(bz[:], gru_bz).then_inc(small_land, 16)
            sp.dma_start(bh[:], gru_bh).then_inc(small_land, 16)
            sp.dma_start(wgs[:], wg).then_inc(small_land, 16)
            sp.dma_start(b2r[:], tok_b2.to_broadcast([P, D])).then_inc(small_land, 16)
            sp.dma_start(stage[:, 1, :], tok_w2.rearrange("p k n -> p (k n)")).then_inc(stage_land[1], 16)
            sp.dma_start(stage[:, 2, 0:GW], gru_wz.rearrange("p l k n -> p (l k n)")).then_inc(stage_land[2], 16)
            sp.dma_start(stage[:, 2, GW:2 * GW], gru_wh.rearrange("p l k n -> p (l k n)")).then_inc(stage_land[2], 16)
            sp.wait_ge(zero_set, 1)
            sp.wait_ge(qT_ps, 1)
            with sp.Fori(0, XT) as j:
                sp.dma_start(x_sorted[bass.ds(j * P, P), :], zero_row[:]).then_inc(zeroed, 16)
            sp.wait_ge(w1_lo, 2)
            sp.dma_start(stage[:, 0, :], w1s).then_inc(stage_land[0], 16)
            sp.wait_ge(w2_lo, 1)
            sp.dma_start(stage[:, 1, :], w2s).then_inc(stage_land[1], 16)
            sp.wait_ge(gru_lo, 1)
            sp.dma_start(stage[:, 2, :], w3s).then_inc(stage_land[2], 16)

            sp.wait_ge(xn2_done, TILES)
            sp.dma_start(x_row[:], xn2[:, 0, :]).then_inc(x_land, 16)
            with sp.Fori(1, FRONT) as i:
                sp.wait_ge(x_ps, i)
                sp.dma_start(x_row[:], xn2[:, bass.ds(i, 1), :].rearrange("p a d -> p (a d)")).then_inc(x_land, 16)
            sp.wait_ge(scattered, 16 * TILES)
            for j in range(3):
                sp.wait_ge(x_ps, FRONT + j)
                sp.dma_start(x_row[:], x_sorted[j * P:(j + 1) * P, :]).then_inc(x_land, 16)
            with sp.Fori(3, XT) as j:
                sp.wait_ge(x_ps, j + FRONT)
                sp.dma_start(x_row[:], x_sorted[bass.ds(j * P, P), :]).then_inc(x_land, 16)
                sp.wait_ge(y_taken, j + (FRONT - 2))
                sp.dma_start(y_sorted[bass.ds(j * P - 3 * P, P), :], y_row[:]).then_inc(y_stored, 16)
            for k in range(3):
                sp.wait_ge(x_ps, B0 + k)
                sp.dma_start(x_row[:], xn2[:, FRONT + k, :]).then_inc(x_land, 16)
                j = XT - 3 + k
                sp.wait_ge(y_taken, FRONT + j + 1)
                sp.dma_start(y_sorted[j * P:(j + 1) * P, :], y_row[:]).then_inc(y_stored, 16)
            with sp.Fori(3, BACK) as k:
                sp.wait_ge(x_ps, k + B0)
                sp.dma_start(x_row[:], xn2[:, bass.ds(k + FRONT, 1), :].rearrange("p a d -> p (a d)")).then_inc(x_land, 16)

            out_v = out.rearrange("(t p) d -> p t d", p=P)
            for n, v in enumerate(finishes):
                sp.wait_ge(summed, n + 1)
                sp.dma_start(out_v[:, v, :], fetched[:, v, :]).then_inc(out_stored, 16)
            sp.wait_ge(out_stored, 16 * len(finishes))

        @block.gpsimd
        def _(pool):
            pool.memset(ident[:], 0.0).then_inc(pool_const, 1)
            pool.wait_ge(pool_const, 1)
            pool.affine_select(out=ident[:], in_=ident[:], compare_op=ALU.not_equal, fill=1.0, base=0,
                               pattern=[[-1, P]], channel_multiplier=1).then_inc(pool_const, 1)

            def gather(b):
                for i in range(BT):
                    pool.indirect_dma_start(
                        out=q[:, i, :], out_offset=None, in_=codebook,
                        in_offset=bass.IndirectOffsetOnAxis(ap=idx_sb[:, b * BT + i:b * BT + i + 1], axis=0),
                        bounds_check=codebook.shape[0] - 1, oob_is_err=True).then_inc(q_land[b], 16)

            pool.wait_ge(idx_land, 16)
            gather(0)
            pool.memset(zero_row[:], 0.0).then_inc(zero_set, 1)
            pool.memset(mhalf[:], -0.5).then_inc(pool_const, 1)

            pool.wait_ge(qT_ps, 2)
            gather(1)
            pool.memset(before[:], 1.0).then_inc(pool_const, 1)
            pool.wait_ge(pool_const, 4)
            pool.affine_select(out=before[:], in_=before[:], compare_op=ALU.is_gt, fill=0.0, base=0,
                               pattern=[[1, P]], channel_multiplier=-1).then_inc(pool_const, 1)
            pool.iota(rank8[:], [[0, TILES], [-1, EXPERTS]], base=EXPERTS, channel_multiplier=0,
                      allow_small_or_imprecise_dtypes=True).then_inc(pool_const, 1)
            pool.iota(steps[:], [[0, EXPERTS], [P, TILES]], base=0, channel_multiplier=0,
                      allow_small_or_imprecise_dtypes=True).then_inc(pool_const, 1)
            pool.iota(tile_no[:], [[1, XT], [0, EXPERTS - 1]], base=0, channel_multiplier=0,
                      allow_small_or_imprecise_dtypes=True).then_inc(pool_const, 1)

            norms = [0]

            def rstd_of(done, need, half):
                n = norms[0]
                norms[0] += 1
                pool.wait_ge(done, need)
                if n == 0:
                    pool.wait_ge(pool_const, 3)
                else:
                    pool.wait_ge(rstd_done, n)
                pool.tensor_scalar(veps[:], mv[:, half * BT:(half + 1) * BT, 1], EPS, None, ALU.add).then_inc(veps_done, 1)
                pool.wait_ge(veps_done, n + 1)
                pool.tensor_tensor(rstd[:, n * BT:(n + 1) * BT], veps[:], mhalf[:], ALU.pow).then_inc(rstd_done, 1)

            for b in range(BLOCKS):
                if b + 2 < BLOCKS:
                    pool.wait_ge(qT_ps, 2 * (b + 2))
                    gather(b + 2)
                rstd_of(mv_done, (b + 1) * BT, b % 2)

            def split(s, slot):
                for c in range(3):
                    o = slot * SLOT + c * WCH
                    hi = w_slots[:, o:o + WCH]
                    if s == 0:
                        pool.wait_ge(stage_land[c], 32 if c < 2 else 48)
                    else:
                        pool.wait_ge(expert_land[c], 16 * s)
                    pool.tensor_scalar(hi, stage[:, c, :], 1.0, 1.0, ALU.mult, ALU.mult).then_inc(split_hi, 1)
                    pool.wait_ge(split_hi, s * 3 + c + 1)
                    pool.tensor_tensor(w_slots[:, o + PART:o + PART + WCH], stage[:, c, :], f32(hi),
                                       ALU.subtract).then_inc(split_lo, 1)
                    pool.wait_ge(split_lo, s * 3 + c + 1)
                    load(s, c)

            def load(e, c):
                src = (ew1, ew2, ew3)[c]
                if isinstance(e, int):
                    pool.dma_start(stage[:, c, :], src[e]).then_inc(expert_land[c], 16)
                else:
                    pool.dma_start(stage[:, c, :], src[bass.ds(e, 1)].rearrange("a p n -> p (a n)")).then_inc(expert_land[c], 16)

            split(0, 0)
            for n, b in enumerate(block_order):
                rstd_of(mv2_done, (n + 1) * BT, n % 2)
            pool.wait_ge(xl_ps, TILES // 2)
            split(1, 1)

            pool.wait_ge(placed, 1)
            pool.wait_ge(zeroed, 16 * XT)
            for t in range(TILES):
                pool.indirect_dma_start(
                    out=x_sorted, out_offset=bass.IndirectOffsetOnAxis(ap=pos[:, t:t + 1], axis=0),
                    in_=xn2[:, t, :], in_offset=None,
                    bounds_check=XT * P - 1, oob_is_err=True).then_inc(scattered, 16)

            with pool.Fori(2, EXPERTS) as e:
                for c in range(3):
                    pool.wait_ge(split_lo, e * 3 + (c + 1))
                    pool.sem_inc(pool_turn, 1)
                    load(e, c)
            for c, src in enumerate((w1s, w2s, w3s)):
                pool.wait_ge(split_lo, EXPERTS * 3 + c + 1)
                pool.dma_start(stage[:, c, :], src).then_inc(expert_land[c], 16)

            pool.wait_ge(split_lo, 3 * SPLITS)
            pool.wait_ge(y_stored, 16 * XT)
            for t in range(TILES):
                pool.indirect_dma_start(
                    out=fetched[:, t, :], out_offset=None, in_=y_sorted,
                    in_offset=bass.IndirectOffsetOnAxis(ap=pos[:, t:t + 1], axis=0),
                    bounds_check=XT * P - 1, oob_is_err=True).then_inc(fetch_land, 16)

        @block.tensor
        def _(pe):
            def q_transposes(b):
                pe.wait_ge(q_land[b], 16 * BT)
                if b == 0:
                    pe.wait_ge(pool_const, 2)
                elif b == 1:
                    pe.wait_ge(qT_lo, 2)
                else:
                    pe.wait_ge(x1_lo, 2 * (b - 1))
                for k in range(KD):
                    for i in range(BT):
                        last = pe.transpose(ps[:, flip_banks[k], i * P:(i + 1) * P], q[:, i, k * P:(k + 1) * P], ident[:])
                    last.then_inc(qT_ps, 1)

            def mlp_up(b):
                pe.wait_ge(qT_lo, 2 * (b + 1))
                for h in range(HC):
                    n = b * HC + h
                    if n == 0:
                        pe.wait_ge(w1_lo, 1)
                    if n == HC // 2:
                        pe.wait_ge(w1_lo, 2)
                    if n >= len(up_banks):
                        pe.wait_ge(h_lo, n - len(up_banks) + 1)
                    for k in range(KD):
                        cols = slice(h * P, (h + 1) * P)
                        last = mm3(pe, ps[:, up_banks[n % len(up_banks)], :], w1p[:, 0, k, cols], w1p[:, 1, k, cols],
                                   qTp[:, 0, k, :], qTp[:, 1, k, :], k == 0, k == KD - 1)
                    last.then_inc(h_ps, 1)
                    if b and h == FLIP_AFTER:
                        x_transposes(b - 1, flip_banks)

            def x_transposes(b, banks):
                pe.wait_ge(xn_done, BT * (b + 1))
                if banks == flip_banks:
                    pe.wait_ge(qT_lo, 2 * (b + 2))
                else:
                    pe.wait_ge(rec_done, TILES)
                for k in range(KD):
                    for i in range(BT):
                        last = pe.transpose(ps[:, banks[k], i * P:(i + 1) * P], xnb[:, i, k * P:(k + 1) * P], ident[:])
                    last.then_inc(xT_ps, 1)

            def mlp_down(b):
                pe.wait_ge(h_lo, HC * (b + 1))
                if b == 0:
                    pe.wait_ge(w2_lo, 1)
                for i in range(BT):
                    t = b * BT + i
                    if t >= 2:
                        pe.wait_ge(rec_done, t - 1)
                    for h in range(HC):
                        cols = slice(i * P, (i + 1) * P)
                        last = mm3(pe, ps[:, rec_banks[t % 2], 0:D], hTp[:, 0, h, cols], hTp[:, 1, h, cols],
                                   w2p[:, 0, h, :], w2p[:, 1, h, :], h == 0, h == HC - 1)
                    last.then_inc(rec_ps, 1)

            q_transposes(0)
            for b in range(BLOCKS):
                mlp_up(b)
                if b + 1 < BLOCKS:
                    q_transposes(b + 1)
                mlp_down(b)

            def gru(u):
                layer, b, hc = units[u]
                cols = slice(b * NB, (b + 1) * NB)
                if layer == 0:
                    src = lambda part, k: (x1hi, x1lo)[part][:, k, cols]
                    pe.wait_ge(x1_lo, 2 * (b + 1))
                else:
                    src = lambda part, k: h0p[:, part, k, cols]
                    pe.wait_ge(h0_lo, last_unit[0, b] + 1)
                if u == 0:
                    pe.wait_ge(gru_lo, 1)
                if u == 1:
                    pe.wait_ge(rec_done, TILES)
                if u >= RG:
                    pe.wait_ge(scanned, u - RG + 1)
                for g, done in enumerate((k_ps, p_ps)):
                    for k in range(KD):
                        w = slice(hc * P, (hc + 1) * P)
                        last = mm3(pe, ps[:, 2 * (u % RG) + g, :], gruw[:, 0, g, layer, k, w], gruw[:, 1, g, layer, k, w],
                                   src(0, k), src(1, k), k == 0, k == KD - 1)
                    last.then_inc(done, 1)

            def state_transposes(n):
                b = block_order[n]
                pe.wait_ge(scanned, last_unit[1, b] + 1)
                if n == 0:
                    pe.wait_ge(x1_lo, 2 * BLOCKS)
                for i in range(BT):
                    if n:
                        pe.wait_ge(res_done, (n - 1) * BT + i // 2 * 2 + 2)
                    for k in range(KD):
                        t = b * BT + i
                        last = pe.transpose(ps[:, 6 + i // 2, (i % 2) * D + k * P:(i % 2) * D + (k + 1) * P],
                                            h1[:, k, t * P:(t + 1) * P], ident[:])
                    if i % 2:
                        last.then_inc(h1T_ps, 1)

            for u in range(len(units)):
                gru(u)
                if u == KD - 1:
                    x_transposes(BLOCKS - 1, late_banks)
                n = (u - U0) // KD - 1
                if u >= U0 and (u - U0) % KD == KD - 1 and n >= 0:
                    state_transposes(n)
            state_transposes(BLOCKS - 1)

            for b in range(BLOCKS):
                for i in range(BT):
                    n = b * BT + i
                    t = block_order[b] * BT + i
                    pe.wait_ge(xn2_done, n + 1)
                    if n == BT * (BLOCKS - 1):
                        pe.wait_ge(res_done, TILES)
                    for k in range(KD):
                        at_ = (n % 2) * D + k * P
                        last = pe.transpose(ps[:, n // 2, at_:at_ + P], xn2[:, t, k * P:(k + 1) * P], ident[:])
                    if n % 2:
                        last.then_inc(xl_ps, 1)
            pe.wait_ge(small_land, 80)
            pe.wait_ge(xl_act, TILES // 4)
            pe.wait_ge(xl_dve, TILES // 4)
            for t in range(TILES):
                for k in range(KD):
                    last = pe.matmul(ps[:, 7, t * EXPERTS:(t + 1) * EXPERTS], xlT[:, t, k, :], wgs[:, k, :],
                                     start=(k == 0), stop=(k == KD - 1))
            last.then_inc(logit_ps, 1)

            def up(i, slot):
                pe.wait_ge(xT_lo, i + 1)
                for n in range(NH):
                    for w, (bank, done) in enumerate(((0, a_ps), (2, b_ps))):
                        for k in range(KD):
                            o = w * WCH + k * HID + n * NB
                            last = mm3(pe, ps[:, bank + n, :], xTp[:, 0, k, :], xTp[:, 1, k, :],
                                       w_slots[:, bass.ds(slot + o, NB)], w_slots[:, bass.ds(slot + (o + PART), NB)],
                                       k == 0, k == KD - 1)
                        last.then_inc(done, 1)

            def row_transposes(i):
                pe.wait_ge(x_land, 16 * (i + 1))
                for k in range(KD):
                    last = pe.transpose(ps[:, 6, k * P:(k + 1) * P], x_row[:, k * P:(k + 1) * P], ident[:])
                last.then_inc(x_ps, 1)

            def down(i, slot):
                pe.wait_ge(gT_lo, 2 * (i + 1))
                for c in range(HC):
                    o = 2 * WCH + c * D
                    last = mm3(pe, ps[:, 7, 0:D], gTp[:, 0, c, :], gTp[:, 1, c, :],
                               w_slots[:, bass.ds(slot + o, D)], w_slots[:, bass.ds(slot + (o + PART), D)],
                               c == 0, c == HC - 1)
                last.then_inc(tile_done, 1)

            def g_transposes(i):
                for n in range(NH):
                    pe.wait_ge(g_done, 2 * i + n + 1)
                    for c in range(HC // NH):
                        j = n * (HC // NH) + c
                        last = pe.transpose(ps[:, 4 + n, c * P:(c + 1) * P], g_buf[:, j * P:(j + 1) * P], ident[:])
                    last.then_inc(gT_ps, 1)

            pe.wait_ge(split_lo, 3)
            row_transposes(0)
            up(0, 0)
            row_transposes(1)
            pe.wait_ge(onehot_done, 1)
            pe.wait_ge(pool_const, 8)
            pe.wait_ge(dve_const, 1)
            oh = onehot[:].rearrange("p t e -> p (t e)")
            pe.matmul(ps[:, 7, 0:TE], before[:], oh, start=True, stop=True)
            pe.matmul(ps[:, 7, TE:2 * TE], ones[:], oh, start=True, stop=True).then_inc(rank_ps, 1)
            g_transposes(0)
            pe.wait_ge(router, 1)
            up(1, 0)
            row_transposes(2)
            down(0, 0)
            g_transposes(1)
            with pe.Fori(2, FRONT) as i:
                up(i, 0)
                row_transposes(i + 1)
                pe.wait_ge(y_taken, i - 1)
                down(i - 1, 0)
                g_transposes(i)
            pe.wait_ge(routed, 1)

            def split_of(i):
                return pe.value_load(turns[0:1, bass.ds(i, 1)], min_val=0, max_val=2 * SPLITS) >> 1

            with pe.Fori(FRONT, B0) as i:
                before_, here = split_of(i - 1), split_of(i)
                pe.wait_ge(split_lo, here * 3 + 2)
                up(i, (here & 1) * SLOT)
                row_transposes(i + 1)
                pe.wait_ge(y_taken, i - 1)
                pe.wait_ge(split_lo, before_ * 3 + 3)
                down(i - 1, (before_ & 1) * SLOT)
                g_transposes(i)
            before_ = split_of(B0 - 1)
            pe.wait_ge(split_lo, 3 * SPLITS - 1)
            up(B0, SLOT)
            row_transposes(B0 + 1)
            pe.wait_ge(y_taken, B0 - 1)
            pe.wait_ge(split_lo, 3 * SPLITS)
            down(B0 - 1, (before_ & 1) * SLOT)
            g_transposes(B0)
            with pe.Fori(B0 + 1, LT - 1) as i:
                up(i, SLOT)
                row_transposes(i + 1)
                pe.wait_ge(y_taken, i - 1)
                down(i - 1, SLOT)
                g_transposes(i)
            up(LT - 1, SLOT)
            pe.wait_ge(y_taken, LT - 2)
            down(LT - 2, SLOT)
            g_transposes(LT - 1)
            pe.wait_ge(y_taken, LT - 1)
            down(LT - 1, SLOT)

        @block.scalar
        def _(act):
            w1v = stage[:, 0, :].rearrange("p (k n) -> p k n", k=KD)
            act.preload_act_table(ACT.Gelu_apprx_tanh)
            act.wait_ge(stage_land[0], 16)
            for h in range(2):
                cols = slice(h * NB, (h + 1) * NB)
                act.activation(w1p[:, 0, :, cols], w1v[:, :, cols], ACT.Copy).then_inc(w1_hi, 1)
            act.wait_ge(stage_land[1], 16)
            act.activation(w2p[:, 0].rearrange("p k n -> p (k n)"), stage[:, 1, :], ACT.Copy).then_inc(w2_hi, 1)

            def q_hi(b):
                for k in range(KD):
                    act.wait_ge(qT_ps, 2 * b + k + 1)
                    act.activation(qTp[:, 0, k, :], ps[:, flip_banks[k], :], ACT.Copy).then_inc(qT_hi, 1)

            def x_hi(b, banks):
                for k in range(KD):
                    act.wait_ge(xT_ps, 2 * b + k + 1)
                    act.activation(x1hi[:, k, b * NB:(b + 1) * NB], ps[:, banks[k], :], ACT.Copy).then_inc(x1_hi, 1)

            q_hi(0)
            act.wait_ge(stage_land[2], 32)
            act.activation(gruw[:, 0].rearrange("p g l k n -> p (g l k n)"), stage[:, 2, :], ACT.Copy).then_inc(gru_hi, 1)
            act.wait_ge(small_land, 80)
            for b in range(BLOCKS):
                for h in range(HC):
                    n = b * HC + h
                    act.wait_ge(h_ps, n + 1)
                    act.activation(ps[:, up_banks[n % len(up_banks)], :], ps[:, up_banks[n % len(up_banks)], :], ACT.Gelu_apprx_tanh,
                                   bias=b1[:, h:h + 1]).then_inc(h_gelu, 1)
                    act.wait_ge(h_gelu, n + 1)
                    act.activation(hTp[:, 0, h, :], ps[:, up_banks[n % len(up_banks)], :], ACT.Copy).then_inc(h_hi, 1)
                    if b and h == FLIP_AFTER:
                        x_hi(b - 1, flip_banks)
                if b + 1 < BLOCKS:
                    q_hi(b + 1)

            def state_hi(u):
                _, b, hc = units[u]
                act.wait_ge(scanned, u + 1)
                act.activation(h0p[:, 0, hc, b * NB:(b + 1) * NB], h_full[:, u % HF, :], ACT.Copy).then_inc(h0_hi, 1)

            act.preload_act_table(ACT.Sigmoid)
            act.wait_ge(dve_const, 1)
            for u, (layer, b, hc) in enumerate(units):
                c = layer * KD + hc
                bank = 2 * (u % RG)
                act.wait_ge(k_ps, u + 1)
                act.activation(a_gate[:, u % RG, :], ps[:, bank, :], ACT.Sigmoid, bias=nbz[:, c:c + 1],
                               scale=-1.0).then_inc(gates, 1)
                act.activation(ps[:, bank, :], ps[:, bank, :], ACT.Sigmoid, bias=bz[:, c:c + 1]).then_inc(gates, 1)
                act.wait_ge(p_ps, u + 1)
                act.activation(v_gate[:, u % RG, :], ps[:, bank + 1, :], ACT.Sigmoid,
                               bias=bh[:, c:c + 1]).then_inc(gates, 1)
                if 1 <= u <= U0:
                    state_hi(u - 1)
                if u == KD - 1:
                    x_hi(BLOCKS - 1, late_banks)

            act.preload_act_table(ACT.Gelu)
            for m in range(0, TILES // 2, 2):
                t = block_order[2 * m // BT] * BT + 2 * m % BT
                act.wait_ge(xl_ps, m + 1)
                act.activation(xlT[:, t:t + 2, :, :].rearrange("p t k n -> p (t k n)"), ps[:, m, :], ACT.Copy).then_inc(xl_act, 1)

            def row_hi(i):
                act.wait_ge(x_ps, i + 1)
                act.activation(xTp[:, 0, :, :].rearrange("p k n -> p (k n)"), ps[:, 6, 0:D], ACT.Copy).then_inc(xT_hi, 1)

            def tile(i, split=lambda c: None, last=False):
                for n in range(NH):
                    act.wait_ge(a_ps, 2 * i + n + 1)
                    act.activation(gelu_buf[:, n, :], ps[:, n, :], ACT.Gelu).then_inc(gelu_done, 1)
                    if n == 0:
                        split(0)
                if not last:
                    row_hi(i + 1)
                split(1)
                for n in range(NH):
                    act.wait_ge(gT_ps, 2 * i + n + 1)
                    act.activation(gTp[:, 0, n * BT:(n + 1) * BT, :].rearrange("p c n -> p (c n)"), ps[:, 4 + n, :],
                                   ACT.Copy).then_inc(gT_hi, 1)
                split(2)

            row_hi(0)
            with act.Fori(0, FRONT) as i:
                tile(i)
            act.wait_ge(routed, 1)
            with act.Fori(FRONT, B0) as i:
                turn = act.value_load(turns[0:1, bass.ds(i, 1)], min_val=0, max_val=2 * SPLITS)
                s = turn >> 1

                def next_hi(c):
                    with act.If((turn & 1) > 0):
                        act.wait_ge(expert_land[c], s * 16 + 16)
                        act.sem_inc(act_turn, 1)
                        act.activation(w_slots[:, bass.ds(((s + 1) & 1) * SLOT + c * WCH, WCH)], stage[:, c, :],
                                       ACT.Copy).then_inc(split_hi, 1)

                tile(i, next_hi)
            with act.Fori(B0, LT - 1) as i:
                tile(i)
            tile(LT - 1, last=True)

        @block.vector
        def _(dve):
            w1v = stage[:, 0, :].rearrange("p (k n) -> p k n", k=KD)
            for h in range(2):
                cols = slice(h * NB, (h + 1) * NB)
                dve.wait_ge(w1_hi, h + 1)
                dve.tensor_tensor(w1p[:, 1, :, cols], w1v[:, :, cols], f32(w1p[:, 0, :, cols]), ALU.subtract).then_inc(w1_lo, 1)

            def q_lo(b):
                for k in range(KD):
                    dve.wait_ge(qT_hi, 2 * b + k + 1)
                    dve.tensor_tensor(qTp[:, 1, k, :], ps[:, flip_banks[k], :], f32(qTp[:, 0, k, :]), ALU.subtract).then_inc(qT_lo, 1)

            def x_lo(b, banks):
                for k in range(KD):
                    cols = slice(b * NB, (b + 1) * NB)
                    dve.wait_ge(x1_hi, 2 * b + k + 1)
                    dve.tensor_tensor(x1lo[:, k, cols], ps[:, banks[k], :], f32(x1hi[:, k, cols]), ALU.subtract).then_inc(x1_lo, 1)

            def moments(source, n, half, waited, bn, mvs):
                i = n % BT
                dve.wait_ge(waited, n + 1)
                dve.bn_stats(stats[:, i, :], source).then_inc(bn, 1)
                dve.wait_ge(bn, n + 1)
                dve.bn_aggr(mv[:, half * BT + i, :], stats[:, i, :]).then_inc(mvs, 1)

            def normed(dst, source, n, half, i, done):
                m = half * BT + i
                return dve.tensor_scalar(dst, source, mv[:, m, 0:1], rstd[:, n * BT + i:n * BT + i + 1],
                                         ALU.subtract, ALU.mult).then_inc(done, 1)

            def x_norm(b, i):
                if i == 0:
                    dve.wait_ge(rstd_done, b + 1)
                    if b:
                        dve.wait_ge(xT_ps, 2 * b)
                normed(xnb[:, i, :], res[:, b * BT + i, :], b, b % 2, i, xn_done)

            dve.wait_ge(w2_hi, 1)
            dve.tensor_tensor(w2p[:, 1].rearrange("p k n -> p (k n)"), stage[:, 1, :],
                              f32(w2p[:, 0].rearrange("p k n -> p (k n)")), ALU.subtract).then_inc(w2_lo, 1)
            q_lo(0)
            dve.wait_ge(gru_hi, 1)
            dve.tensor_tensor(gruw[:, 1].rearrange("p g l k n -> p (g l k n)"), stage[:, 2, :],
                              f32(gruw[:, 0].rearrange("p g l k n -> p (g l k n)")), ALU.subtract).then_inc(gru_lo, 1)
            dve.wait_ge(small_land, 80)
            for b in range(BLOCKS):
                for h in range(HC):
                    n = b * HC + h
                    if b and h < BT:
                        x_norm(b - 1, h)
                    dve.wait_ge(h_hi, n + 1)
                    dve.tensor_tensor(hTp[:, 1, h, :], ps[:, up_banks[n % len(up_banks)], :], f32(hTp[:, 0, h, :]), ALU.subtract).then_inc(h_lo, 1)
                    if b and h == FLIP_AFTER:
                        x_lo(b - 1, flip_banks)
                if b + 1 < BLOCKS:
                    q_lo(b + 1)
                if b == 0:
                    dve.memset(ones[:], 1.0)
                    dve.tensor_scalar(nbz[:], bz[:], -1.0, None, ALU.mult)
                    dve.tensor_scalar(bh5[:], bh[:], 0.5, None, ALU.add).then_inc(dve_const, 1)
                for i in range(BT):
                    t = b * BT + i
                    dve.wait_ge(rec_ps, t + 1)
                    dve.tensor_tensor(res[:, t, :], ps[:, rec_banks[t % 2], 0:D], b2r[:], ALU.add).then_inc(rec_done, 1)
                    moments(res[:, t, :], t, b % 2, rec_done, bn_done, mv_done)

            for i in range(BT):
                x_norm(BLOCKS - 1, i)

            def residual(n):
                for i in range(BT):
                    t = block_order[n] * BT + i
                    m = n * BT + i
                    dve.wait_ge(h1T_ps, m // 2 + 1)
                    dve.tensor_tensor(res[:, t, :], ps[:, 6 + i // 2, (i % 2) * D:(i % 2 + 1) * D], res[:, t, :],
                                      ALU.add).then_inc(res_done, 1)
                    moments(res[:, t, :], m, n % 2, res_done, bn2_done, mv2_done)

            def x2_norm(n):
                dve.wait_ge(rstd_done, BLOCKS + n + 1)
                for i in range(BT):
                    t = block_order[n] * BT + i
                    normed(xn2[:, t, :], res[:, t, :], BLOCKS + n, n % 2, i, xn2_done)

            def state_lo(u):
                _, b, hc = units[u]
                cols = slice(b * NB, (b + 1) * NB)
                dve.wait_ge(h0_hi, u + 1)
                dve.tensor_tensor(h0p[:, 1, hc, cols], h_full[:, u % HF, :], f32(h0p[:, 0, hc, cols]),
                                  ALU.subtract).then_inc(h0_lo, 1)

            carries = 0
            dve.wait_ge(dve_const, 1)
            for u, (layer, b, hc) in enumerate(units):
                c = layer * KD + hc
                bank = 2 * (u % RG)
                g = v_gate[:, u % RG, :]
                dve.wait_ge(gates, 3 * u + 3)
                dve.scalar_tensor_tensor(out=g, in0=ps[:, bank + 1, :], scalar=bh5[:, c:c + 1], in1=g, op0=ALU.add,
                                         op1=ALU.max).then_inc(gate_steps, 1)
                dve.wait_ge(gate_steps, 2 * u + 1)
                dve.tensor_tensor(g, ps[:, bank, :], g, ALU.mult).then_inc(gate_steps, 1)
                if u == KD - 1:
                    x_lo(BLOCKS - 1, late_banks)
                dve.wait_ge(gate_steps, 2 * u + 2)
                first_block = b % SB == 0
                if layer == 0:
                    if u >= HF:
                        dve.wait_ge(h0_lo, u - HF + 1)
                    h = h_full[:, u % HF, :]
                    m = (b // SB) * KD + hc
                    init = H0 if first_block else carry[:, m:m + 1]
                    if not first_block:
                        dve.wait_ge(carried, carries)
                else:
                    h = h1[:, hc, b * NB:(b + 1) * NB]
                    init = H0 if first_block else h1[:, hc, b * NB - 1:b * NB]
                    if not first_block:
                        dve.wait_ge(scanned, last_unit[1, b - 1] + 1)
                dve.tensor_tensor_scan(h, a_gate[:, u % RG, :], g, init, ALU.mult, ALU.add).then_inc(scanned, 1)
                if layer == 0 and first_block:
                    dve.wait_ge(scanned, u + 1)
                    dve.tensor_copy(carry[:, m:m + 1], h[:, NB - 1:NB]).then_inc(carried, 1)
                    carries += 1
                if 1 <= u <= U0:
                    state_lo(u - 1)
                n = (u - U0) // KD - 1
                if u >= U0 and (u - U0) % KD == KD - 1 and n >= 0:
                    residual(n)
                    if n:
                        x2_norm(n - 1)
            residual(BLOCKS - 1)
            x2_norm(BLOCKS - 2)
            x2_norm(BLOCKS - 1)

            for m in range(1, TILES // 2, 2):
                t = block_order[2 * m // BT] * BT + 2 * m % BT
                dve.wait_ge(xl_ps, m + 1)
                dve.tensor_copy(xlT[:, t:t + 2, :, :].rearrange("p t k n -> p (t k n)"), ps[:, m, :]).then_inc(xl_dve, 1)

            steps_done = [0]

            def step(ins):
                steps_done[0] += 1
                ins.then_inc(router, 1)
                dve.wait_ge(router, steps_done[0])

            def over_experts(ap):
                return ap.unsqueeze(2).to_broadcast([P, TILES, EXPERTS])

            dve.wait_ge(logit_ps, 1)
            dve.wait_ge(pool_const, 8)
            chosen = [0]

            def choose(ins):
                chosen[0] += 1
                ins.then_inc(onehot_steps, 1)
                dve.wait_ge(onehot_steps, chosen[0])

            choose(dve.tensor_copy(logits[:].rearrange("p t e -> p (t e)"), ps[:, 7, 0:TE]))
            choose(dve.tensor_reduce(best[:], logits[:], AX, ALU.max))
            choose(dve.tensor_tensor(score[:], logits[:], over_experts(best[:]), ALU.is_ge))
            choose(dve.tensor_tensor(score[:], score[:], rank8[:], ALU.mult))
            choose(dve.tensor_reduce(first[:], score[:], AX, ALU.max))
            dve.tensor_tensor(onehot[:], rank8[:], over_experts(first[:]), ALU.is_equal).then_inc(onehot_done, 1)

            def row_lo(i):
                dve.wait_ge(xT_hi, i + 1)
                dve.tensor_tensor(xTp[:, 1, :, :].rearrange("p k n -> p (k n)"), ps[:, 6, 0:D],
                                  f32(xTp[:, 0, :, :].rearrange("p k n -> p (k n)")), ALU.subtract).then_inc(xT_lo, 1)

            def gated_half(i, n):
                dve.wait_ge(gelu_done, 2 * i + n + 1)
                dve.wait_ge(b_ps, 2 * i + n + 1)
                dve.tensor_tensor(g_buf[:, n * NB:(n + 1) * NB], ps[:, 2 + n, :], gelu_buf[:, n, :],
                                  ALU.mult).then_inc(g_done, 1)

            def gated(i):
                for n in range(NH):
                    gated_half(i, n)

            def gated_lo(i):
                for n in range(NH):
                    half = slice(n * BT, (n + 1) * BT)
                    dve.wait_ge(gT_hi, 2 * i + n + 1)
                    dve.tensor_tensor(gTp[:, 1, half, :].rearrange("p c n -> p (c n)"), ps[:, 4 + n, :],
                                      f32(gTp[:, 0, half, :].rearrange("p c n -> p (c n)")), ALU.subtract).then_inc(gT_lo, 1)

            def add_shared(i, t):
                r = res[:, bass.ds(t, 1), :].rearrange("p a d -> p (a d)")
                dve.wait_ge(tile_done, i + 1)
                dve.tensor_tensor(r, ps[:, 7, 0:D], r, ALU.add).then_inc(y_taken, 1)

            row_lo(0)
            gated(0)
            row_lo(1)
            dve.wait_ge(rank_ps, 1)
            dve.tensor_copy(ranks[:].rearrange("p a n -> p (a n)"), ps[:, 7, 0:2 * TE]).then_inc(router, 1)
            steps_done[0] = 1
            gated_lo(0)

            dve.wait_ge(router, 1)
            step(dve.tensor_copy(totals[:], ranks[:, 1, :].rearrange("p (t e) -> p e t", e=EXPERTS)))
            flat = totals[:].rearrange("p e t -> p (e t)")
            step(dve.tensor_tensor_scan(upto[:], ones[:, 0:TE], flat, 0.0, ALU.mult, ALU.add))
            step(dve.tensor_tensor(upto[:], upto[:], flat, ALU.subtract))
            step(dve.tensor_reduce(counts[:], totals[:], AX, ALU.add))
            step(dve.memset(steps[:, :, 0:1], -1.0))
            step(dve.tensor_tensor(over[:], counts[:].unsqueeze(2).to_broadcast([P, EXPERTS, TILES]), steps[:], ALU.is_gt))
            step(dve.tensor_reduce(tiles_e[:], over[:], AX, ALU.add))
            step(dve.tensor_tensor_scan(tiles_upto[:], ones[:, 0:EXPERTS], tiles_e[:], 0.0, ALU.mult, ALU.add))
            step(dve.tensor_tensor(first_row[:], tiles_upto[:], tiles_e[:], ALU.subtract))
            upto_v = upto[:].rearrange("p (e t) -> p e t", e=EXPERTS)
            step(dve.scalar_tensor_tensor(out=shift[:], in0=first_row[:], scalar=float(P), in1=upto_v[:, :, 0],
                                          op0=ALU.mult, op1=ALU.subtract))
            step(dve.tensor_tensor(base[:], upto_v, shift[:].unsqueeze(2).to_broadcast([P, EXPERTS, TILES]), ALU.add))
            step(dve.tensor_tensor(place_te[:], ranks[:, 0, :].rearrange("p (t e) -> p t e", e=EXPERTS),
                                   base[:].rearrange("p e t -> p t e"), ALU.add))
            step(dve.tensor_tensor(place_te[:], place_te[:], onehot[:], ALU.mult))
            step(dve.tensor_reduce(pos_f[:], place_te[:], AX, ALU.add))
            dve.tensor_copy(pos[:], pos_f[:]).then_inc(placed, 1)
            upto_b = tiles_upto[:, 0:EXPERTS - 1].unsqueeze(1).to_broadcast([P, XT, EXPERTS - 1])
            step(dve.tensor_tensor(past[:], tile_no[:], upto_b, ALU.is_ge))
            step(dve.tensor_reduce(expert_f[:], past[:], AX, ALU.add))
            step(dve.memset(fresh[:, 0:1], 1.0))
            step(dve.tensor_tensor(fresh[:, 1:XT], expert_f[:, 1:XT], expert_f[:, 0:XT - 1], ALU.subtract))
            step(dve.tensor_scalar(expert_f[:], expert_f[:], 2.0, 2.0, ALU.mult, ALU.add))
            step(dve.memset(turns[:, 0:FRONT], 0))
            step(dve.tensor_tensor(turns[:, FRONT:B0], expert_f[:], fresh[:], ALU.add))
            dve.memset(stats[:, 0, 0:1], 0.0).then_inc(routed, 1)

            with dve.Fori(1, FRONT) as i:
                gated(i)
                row_lo(i + 1)
                add_shared(i - 1, i - 1)
                gated_lo(i)

            def routed_tile(i, take_before):
                turn = dve.value_load(turns[0:1, bass.ds(i, 1)], min_val=0, max_val=2 * SPLITS)
                s = turn >> 1

                def next_lo(c):
                    with dve.If((turn & 1) > 0):
                        to = ((s + 1) & 1) * SLOT
                        dve.wait_ge(split_hi, s * 3 + (c + 4))
                        dve.tensor_tensor(w_slots[:, bass.ds(to + (PART + c * WCH), WCH)], stage[:, c, :],
                                          f32(w_slots[:, bass.ds(to + c * WCH, WCH)]), ALU.subtract).then_inc(split_lo, 1)

                gated_half(i, 0)
                next_lo(0)
                gated_half(i, 1)
                row_lo(i + 1)
                next_lo(1)
                take_before()
                gated_lo(i)
                next_lo(2)

            def take_routed(i, stored=None):
                dve.wait_ge(tile_done, i + 1)
                if stored is not None:
                    dve.wait_ge(y_stored, stored)
                dve.tensor_copy(y_row[:], ps[:, 7, 0:D]).then_inc(y_taken, 1)

            dve.wait_ge(routed, 1)
            routed_tile(FRONT, lambda: add_shared(FRONT - 1, FRONT - 1))
            routed_tile(FRONT + 1, lambda: take_routed(FRONT))
            with dve.Fori(FRONT + 2, B0) as i:
                routed_tile(i, lambda: take_routed(i - 1, 16 * i - 16 * (FRONT + 1)))
            gated(B0)
            row_lo(B0 + 1)
            take_routed(B0 - 1, 16 * (XT - 1))
            gated_lo(B0)

            def finish(n):
                v = finishes[n]
                dve.wait_ge(fetch_land, 16 * TILES)
                dve.wait_ge(y_taken, v.stop if v.stop <= FRONT else v.stop + XT)
                dve.tensor_tensor(fetched[:, v, :], fetched[:, v, :], res[:, v, :], ALU.add).then_inc(summed, 1)

            with dve.Fori(B0 + 1, LT - 2) as i:
                gated(i)
                row_lo(i + 1)
                add_shared(i - 1, i - (XT + 1))
                gated_lo(i)
            for i in (LT - 2, LT - 1):
                gated(i)
                if i < LT - 1:
                    row_lo(i + 1)
                add_shared(i - 1, i - 1 - XT)
                gated_lo(i)
                if i == LT - 2:
                    for n in range(3):
                        finish(n)
                finish(len(finishes) - 1 - LT + i)
            add_shared(LT - 1, TILES - 1)
            finish(len(finishes) - 1)


def kernel(x, L0_tok_codebook, L0_tok_W1, L0_tok_b1, L0_tok_W2, L0_tok_b2, L0_attn_Wz, L0_attn_bz, L0_attn_Wh,
           L0_attn_bh, L0_ffn_w1s, L0_ffn_w2s, L0_ffn_w3s, L0_ffn_W1, L0_ffn_W2, L0_ffn_W3, L0_ffn_Wg):
    import numpy as np
    import concourse.bacc as bacc
    from concourse import mybir as mb
    from concourse.bass_utils import run_bass_kernel_spmd

    def rows(a):
        a = np.asarray(a)
        k, n = a.shape[-2:]
        a = a.reshape(*a.shape[:-2], k // P, P, n)
        return np.swapaxes(a, -3, -2)

    def flat(a):
        a = rows(a)
        return a.reshape(*a.shape[:-2], -1)

    def column(a):
        return np.asarray(a).reshape(-1, P).T

    def gru(a):
        return rows(np.swapaxes(np.asarray(a), 1, 2)).transpose(1, 0, 2, 3)

    x = np.asarray(x)
    data = {
        "idx": x.reshape(-1, P).T,
        "codebook": np.asarray(L0_tok_codebook),
        "tok_w1": rows(L0_tok_W1), "tok_b1": column(L0_tok_b1),
        "tok_w2": rows(L0_tok_W2), "tok_b2": np.asarray(L0_tok_b2).reshape(1, -1),
        "gru_wz": gru(L0_attn_Wz), "gru_bz": column(L0_attn_bz),
        "gru_wh": gru(L0_attn_Wh), "gru_bh": column(L0_attn_bh),
        "w1s": flat(L0_ffn_w1s), "w2s": flat(L0_ffn_w2s), "w3s": flat(L0_ffn_w3s),
        "ew1": flat(L0_ffn_W1), "ew2": flat(L0_ffn_W2), "ew3": flat(L0_ffn_W3),
        "wg": rows(L0_ffn_Wg),
    }
    nc = bacc.Bacc("TRN2", target_bir_lowering=False, num_devices=1)
    arrays, args = {}, {}
    for name, a in data.items():
        a = np.ascontiguousarray(a)
        arrays[name + "_in"] = a
        args[name] = nc.dram_tensor(name + "_in", a.shape, mb.dt.from_np(a.dtype), kind="ExternalInput").ap()
    d = data["codebook"].shape[1]
    args["out"] = nc.dram_tensor("out_rows", (x.size, d), mb.dt.float32, kind="ExternalOutput").ap()
    build(nc, **args)
    r = run_bass_kernel_spmd(nc, [arrays], core_ids=[0])
    return r.results[0]["out_rows"].reshape(*x.shape, d)
```

```python
from contextlib import ExitStack

import concourse.bass as bass
from concourse import mybir

P = 128
ALU = mybir.AluOpType
ACT = mybir.ActivationFunctionType
AX = mybir.AxisListType.X
F32 = mybir.dt.float32
F32R = mybir.dt.float32r
I32 = mybir.dt.int32
U16 = mybir.dt.uint16
EPS = 1e-5
H0 = 0.5


def build(nc, idx, codebook, tok_w1, tok_b1, tok_w2, tok_b2, gru_wz, gru_bz, gru_wh, gru_bh,
          w1s, w2s, w3s, ew1, ew2, ew3, wg, out):
    TILES = idx.shape[1]
    D = codebook.shape[1]
    KD = D // P
    HID = tok_w1.shape[2]
    HC = HID // P
    NB = 512
    BT = NB // P
    BLOCKS = TILES // BT
    LAYERS = gru_wz.shape[1]
    BATCH = 2
    SB = BLOCKS // BATCH
    EXPERTS = ew1.shape[0]
    XT = TILES + EXPERTS - 1
    FRONT = TILES // 2
    PEELED = 4
    BACK = TILES - FRONT
    SURE = FRONT + TILES
    END = FRONT + XT
    SPLITS = EXPERTS + 2
    NH = HID // NB
    WCH = KD * HID
    PART = 3 * WCH
    SLOT = 2 * PART
    GW = LAYERS * KD * D

    x_sorted = nc.dram_tensor("x_sorted", [XT * P, D], F32, kind="Internal").ap()
    y_sorted = nc.dram_tensor("y_sorted", [XT * P, D], F32, kind="Internal").ap()

    with ExitStack() as ctx:
        place = [17 * 1024]

        def at(name, shape, dt, offset):
            return nc.alloc_sbuf_tensor_at(name, shape, dt, offset=offset)

        def region(kib):
            here = place[0]
            place[0] += kib * 1024
            return here

        def small(name, shape, dt=F32):
            size = 4
            for n in shape[1:]:
                size *= n
            here = place[0]
            place[0] += -(-size // 32) * 32
            return at(name, shape, dt, here)

        def sem(name):
            return ctx.enter_context(nc.semaphore(name))

        r_slots = region(96)
        r_stage = region(24)
        r_x1hi = region(16)
        r_x1lo = region(16)
        r_gruw = region(16)
        r_res = region(16)
        K = 1024

        w_slots = at("w_slots", [P, 2 * SLOT], F32R, r_slots)
        w1p = at("w1p", [P, 2, KD, HID], F32R, r_slots)
        w2p = at("w2p", [P, 2, HC, D], F32R, r_slots + 16 * K)
        hTp = at("hTp", [P, 2, HC, NB], F32R, r_slots + 32 * K)
        qTp = at("qTp", [P, 2, KD, NB], F32R, r_slots + 64 * K)
        q = at("q", [P, BT, D], F32, r_slots + 72 * K)
        xnb = at("xnb", [P, BT, D], F32, r_slots + 76 * K)
        h0p = at("h0p", [P, 2, KD, TILES * P], F32R, r_slots + 48 * K)
        RG = 3
        HF = 2
        a_gate = at("a_gate", [P, RG, NB], F32, r_slots + 80 * K)
        v_gate = at("v_gate", [P, RG, NB], F32, r_slots + 86 * K)
        h_full = at("h_full", [P, HF, NB], F32, r_slots + 92 * K)
        xbT = at("xbT", [P, 2, KD, BACK * P], F32R, r_x1lo)
        gb_hi_at = (r_slots, r_gruw)
        gb_lo_at = ((r_slots + 24 * K, r_slots + 32 * K), (r_slots + 16 * K, r_slots + 40 * K))
        gb_hi_of = [at(f"gb_hi{b}", [P, HC, NB], F32R, gb_hi_at[b]) for b in range(2)]
        gb_lo_of = [[at(f"gb_lo{b}{n}", [P, HC // 2, NB], F32R, gb_lo_at[b][n]) for n in range(2)] for b in range(2)]
        gelub = at("gelub", [P, 2, NB], F32, r_stage + 16 * K)
        fetched = at("fetched", [P, TILES, D], F32, r_stage)

        stage = at("stage", [P, 3, WCH], F32, r_stage)
        x1hi = at("x1hi", [P, KD, TILES * P], F32R, r_x1hi)
        x1lo = at("x1lo", [P, KD, TILES * P], F32R, r_x1lo)
        h1 = at("h1", [P, KD, TILES * P], F32, r_x1hi)
        xlT = at("xlT", [P, TILES, KD, P], F32, r_x1hi)
        xn2 = at("xn2", [P, TILES, D], F32, r_x1lo)
        gruw = at("gruw", [P, 2, 2, LAYERS, KD, D], F32R, r_gruw)
        g_buf = at("g_buf", [P, HID], F32, r_gruw)
        gelu_buf = at("gelu_buf", [P, NH, NB], F32, r_gruw + 4 * K)
        gTp = at("gTp", [P, 2, HC, P], F32R, r_gruw + 8 * K)
        res = at("res", [P, TILES, D], F32, r_res)

        ident = small("ident", [P, P])
        before = small("before", [P, P])
        ones = small("ones", [P, P])
        b2r = small("b2r", [P, D])
        x_row = small("x_row", [P, D])
        xTp = small("xTp", [P, 2, KD, P], F32R)
        y_row = small("y_row", [P, D])
        zero_row = small("zero_row", [P, D])
        idx_sb = small("idx_sb", [P, TILES], I32)
        b1 = small("b1", [P, HC])
        bz = small("bz", [P, LAYERS * KD])
        bh = small("bh", [P, LAYERS * KD])
        nbz = small("nbz", [P, LAYERS * KD])
        bh5 = small("bh5", [P, LAYERS * KD])
        wgs = small("wgs", [P, KD, EXPERTS])
        stats = small("stats", [P, BT, 6])
        mv = small("mv", [P, 2 * BT, 2])
        veps = small("veps", [P, BT])
        rstd = small("rstd", [P, 2 * TILES])
        mhalf = small("mhalf", [P, BT])
        carry = small("carry", [P, BATCH * KD])

        TE = TILES * EXPERTS
        logits = small("logits", [P, TILES, EXPERTS])
        best = small("best", [P, TILES])
        rank8 = small("rank8", [P, TILES, EXPERTS])
        score = small("score", [P, TILES, EXPERTS])
        first = small("first", [P, TILES])
        onehot = small("onehot", [P, TILES, EXPERTS])
        ranks = small("ranks", [P, 2, TE])
        totals = small("totals", [P, EXPERTS, TILES])
        upto = small("upto", [P, TE])
        counts = small("counts", [P, EXPERTS])
        steps = small("steps", [P, EXPERTS, TILES])
        over = small("over", [P, EXPERTS, TILES])
        tiles_e = small("tiles_e", [P, EXPERTS])
        tiles_upto = small("tiles_upto", [P, EXPERTS])
        first_row = small("first_row", [P, EXPERTS])
        shift = small("shift", [P, EXPERTS])
        base = small("base", [P, EXPERTS, TILES])
        place_te = small("place_te", [P, TILES, EXPERTS])
        pos_f = small("pos_f", [P, TILES])
        pos = small("pos", [P, TILES], I32)
        tile_no = small("tile_no", [P, XT, EXPERTS - 1])
        past = small("past", [P, XT, EXPERTS - 1])
        expert_f = small("expert_f", [P, XT])
        turns = small("turns", [P, END + 1], U16)
        fresh = small("fresh", [P, XT])

        up_banks = (0, 1, 2, 7)
        rec_banks = (3, 6)
        flip_banks = (4, 5)
        late_banks = (6, 7)
        state_banks = ((6, 7), (6, 7), (4, 5), (4, 5))
        ps = ctx.enter_context(nc.psum_tensor("ps", [P, 8, NB], F32))

        idx_land = sem("idx_land"); small_land = sem("small_land");
        stage_land = [sem(f"stage_land{c}") for c in range(3)]
        expert_land = [sem(f"expert_land{c}") for c in range(3)]
        q_land = [sem(f"q_land{b}") for b in range(BLOCKS)]
        zeroed = sem("zeroed"); y_zeroed = sem("y_zeroed"); zero_set = sem("zero_set")
        pool_const = sem("pool_const"); dve_const = sem("dve_const")
        w1_hi = sem("w1_hi"); w1_lo = sem("w1_lo"); w2_hi = sem("w2_hi"); w2_lo = sem("w2_lo"); gru_hi = sem("gru_hi"); gru_lo = sem("gru_lo")
        qT_ps = sem("qT_ps"); qT_hi = sem("qT_hi"); qT_lo = sem("qT_lo")
        h_ps = sem("h_ps"); h_gelu = sem("h_gelu"); h_hi = sem("h_hi"); h_lo = sem("h_lo")
        rec_ps = sem("rec_ps"); rec_done = sem("rec_done"); bn_done = sem("bn_done"); mv_done = sem("mv_done")
        veps_done = sem("veps_done"); rstd_done = sem("rstd_done"); xn_done = sem("xn_done")
        xT_ps = sem("xT_ps"); x1_hi = sem("x1_hi"); x1_lo = sem("x1_lo")
        k_ps = sem("k_ps"); p_ps = sem("p_ps"); gates = sem("gates"); gate_steps = sem("gate_steps")
        scanned = sem("scanned"); carried = sem("carried"); h0_hi = sem("h0_hi"); h0_lo = sem("h0_lo")
        h1T_ps = sem("h1T_ps"); state_rows = sem("state_rows"); res_done = sem("res_done"); bn2_done = sem("bn2_done"); mv2_done = sem("mv2_done")
        xn2_done = sem("xn2_done"); xl_ps = sem("xl_ps"); xl_act = sem("xl_act"); xl_dve = sem("xl_dve")
        logit_ps = sem("logit_ps"); logits_taken = sem("logits_taken"); onehot_done = sem("onehot_done"); rank_ps = sem("rank_ps"); onehot_steps = sem("onehot_steps")
        router = sem("router"); routed = sem("routed"); scattered = sem("scattered")
        x_land = sem("x_land"); x_ps = sem("x_ps"); xT_hi = sem("xT_hi"); xT_lo = sem("xT_lo")
        a_ps = sem("a_ps"); b_ps = sem("b_ps"); gelu_done = sem("gelu_done"); g_done = sem("g_done")
        gT_ps = sem("gT_ps"); gT_hi = sem("gT_hi"); gT_lo = sem("gT_lo")
        xb_hi = sem("xb_hi"); xb_lo = sem("xb_lo"); ab_ps = sem("ab_ps"); bb_ps = sem("bb_ps")
        gelub_done = sem("gelub_done"); gb_done = sem("gb_done"); gb_hi = sem("gb_hi"); gb_lo = sem("gb_lo")
        rows_ps = sem("rows_ps"); rows_taken = sem("rows_taken")
        tile_done = sem("tile_done"); y_taken = sem("y_taken"); y_stored = sem("y_stored")
        split_hi = sem("split_hi"); pool_turn = sem("pool_turn"); act_turn = sem("act_turn"); placed = sem("placed"); split_lo = sem("split_lo")
        fetch_land = sem("fetch_land")
        presummed = sem("presummed"); summed = sem("summed"); out_stored = sem("out_stored")

        def f32(ap):
            return ap.bitcast(F32)

        def mm3(pe, dst, lhs_hi, lhs_lo, rhs_hi, rhs_lo, start, stop):
            pe.matmul(dst, lhs_hi, rhs_hi, start=start, stop=False)
            pe.matmul(dst, lhs_hi, rhs_lo, start=False, stop=False)
            return pe.matmul(dst, lhs_lo, rhs_hi, start=False, stop=stop)

        units = [(layer, b, hc) for layer in range(LAYERS) for b in range(BLOCKS) for hc in range(KD)]
        U0 = len(units) // LAYERS
        UNITS = len(units)

        def pair(u):
            return 2 * ((u - UNITS) % RG)

        last_unit = {(layer, b): u for u, (layer, b, hc) in enumerate(units)}

        def back_of(engine):
            engine.wait_ge(routed, 1)
            return engine.value_load(turns[0:1, END:END + 1], min_val=0, max_val=END - SURE) + SURE

        finishes = [slice(b * BT, (b + 1) * BT) for b in range(BLOCKS - 1)] + [slice(t, t + 1) for t in range(TILES - BT, TILES)]

        CHUNKS = 2 * HC
        BACK_PAIRS = 3

        def rows_behind(n):
            return (n - HC) // 2 if n > HC and n % 2 else None

        def gb(part, b, h, cols):
            if part == 0:
                return gb_hi_of[b][:, h, cols]
            return gb_lo_of[b][h // (HC // 2)][:, h % (HC // 2), cols]

        FLIP_AFTER = HC // 2 + 1

        block = ctx.enter_context(nc.Block())

        @block.sync
        def _(sp):
            sp.dma_start(idx_sb[:], idx).then_inc(idx_land, 16)
            sp.dma_start(stage[:, 0, :], tok_w1.rearrange("p k n -> p (k n)")).then_inc(stage_land[0], 16)
            sp.dma_start(b1[:], tok_b1).then_inc(small_land, 16)
            sp.dma_start(bz[:], gru_bz).then_inc(small_land, 16)
            sp.dma_start(bh[:], gru_bh).then_inc(small_land, 16)
            sp.dma_start(wgs[:], wg).then_inc(small_land, 16)
            sp.wait_ge(q_land[0], 16 * BT)
            sp.dma_start(b2r[:], tok_b2.to_broadcast([P, D])).then_inc(small_land, 16)
            sp.dma_start(stage[:, 1, :], tok_w2.rearrange("p k n -> p (k n)")).then_inc(stage_land[1], 16)
            sp.dma_start(stage[:, 2, 0:GW], gru_wz.rearrange("p l k n -> p (l k n)")).then_inc(stage_land[2], 16)
            sp.dma_start(stage[:, 2, GW:2 * GW], gru_wh.rearrange("p l k n -> p (l k n)")).then_inc(stage_land[2], 16)
            sp.wait_ge(zero_set, 1)
            sp.wait_ge(qT_ps, 1)
            with sp.Fori(0, XT) as j:
                sp.dma_start(x_sorted[bass.ds(j * P, P), :], zero_row[:]).then_inc(zeroed, 16)
            with sp.Fori(TILES, XT) as j:
                sp.dma_start(y_sorted[bass.ds(j * P, P), :], zero_row[:]).then_inc(y_zeroed, 16)
            sp.wait_ge(w1_lo, 2)
            sp.dma_start(stage[:, 0, :], w1s).then_inc(stage_land[0], 16)
            sp.wait_ge(w2_lo, 1)
            sp.dma_start(stage[:, 1, :], w2s).then_inc(stage_land[1], 16)
            sp.wait_ge(gru_lo, 1)
            sp.dma_start(stage[:, 2, :], w3s).then_inc(stage_land[2], 16)

            for i in range(PEELED, FRONT):
                sp.wait_ge(xn2_done, i + 1)
                if i > PEELED:
                    sp.wait_ge(x_ps, i)
                sp.dma_start(x_row[:], xn2[:, i, :]).then_inc(x_land, 16)
            sp.wait_ge(scattered, 16 * TILES)
            for j in range(3):
                sp.wait_ge(x_ps, FRONT + j)
                sp.dma_start(x_row[:], x_sorted[j * P:(j + 1) * P, :]).then_inc(x_land, 16)
            sp.wait_ge(y_zeroed, 16 * (XT - TILES))

            def sorted_rows(j):
                sp.wait_ge(x_ps, j + FRONT)
                sp.dma_start(x_row[:], x_sorted[bass.ds(j * P, P), :]).then_inc(x_land, 16)
                sp.wait_ge(y_taken, j + (FRONT - 2))
                sp.dma_start(y_sorted[bass.ds(j * P - 3 * P, P), :], y_row[:]).then_inc(y_stored, 16)

            with sp.Fori(3, TILES) as j:
                sorted_rows(j)
            back = back_of(sp)
            with sp.Fori(TILES, XT) as j:
                with sp.If((back - FRONT - j) > 0):
                    sorted_rows(j)
            sp.wait_ge(x_ps, back)
            sp.dma_start(x_row[:], x_sorted[0:P, :]).then_inc(x_land, 16)
            for k in range(3):
                sp.wait_ge(y_taken, back + (k - 2))
                sp.dma_start(y_sorted[bass.ds(back * P + (k - 3 - FRONT) * P, P), :], y_row[:]).then_inc(y_stored, 16)

            out_v = out.rearrange("(t p) d -> p t d", p=P)
            for n, v in enumerate(finishes):
                sp.wait_ge(summed, n + 1)
                sp.dma_start(out_v[:, v, :], fetched[:, v, :]).then_inc(out_stored, 16)
            sp.wait_ge(out_stored, 16 * len(finishes))

        @block.gpsimd
        def _(pool):
            pool.memset(ident[:], 0.0).then_inc(pool_const, 1)
            pool.wait_ge(pool_const, 1)
            pool.affine_select(out=ident[:], in_=ident[:], compare_op=ALU.not_equal, fill=1.0, base=0,
                               pattern=[[-1, P]], channel_multiplier=1).then_inc(pool_const, 1)

            def gather(b):
                for i in range(BT):
                    pool.indirect_dma_start(
                        out=q[:, i, :], out_offset=None, in_=codebook,
                        in_offset=bass.IndirectOffsetOnAxis(ap=idx_sb[:, b * BT + i:b * BT + i + 1], axis=0),
                        bounds_check=codebook.shape[0] - 1, oob_is_err=True).then_inc(q_land[b], 16)

            pool.wait_ge(idx_land, 16)
            gather(0)
            pool.memset(zero_row[:], 0.0).then_inc(zero_set, 1)
            pool.memset(mhalf[:], -0.5).then_inc(pool_const, 1)

            pool.wait_ge(qT_ps, 2)
            gather(1)

            for c, need, parts, hi_done, lo_done in ((1, 16, w2p[:].rearrange("p a k n -> p a (k n)"), w2_hi, w2_lo),
                                                     (2, 32, gruw[:].rearrange("p a g l k n -> p a (g l k n)"), gru_hi, gru_lo)):
                pool.wait_ge(stage_land[c], need)
                pool.tensor_scalar(parts[:, 0], stage[:, c, :], 1.0, 1.0, ALU.mult, ALU.mult).then_inc(hi_done, 1)
                pool.wait_ge(hi_done, 1)
                pool.tensor_tensor(parts[:, 1], stage[:, c, :], f32(parts[:, 0]), ALU.subtract).then_inc(lo_done, 1)

            pool.memset(before[:], 1.0).then_inc(pool_const, 1)
            pool.wait_ge(pool_const, 4)
            pool.affine_select(out=before[:], in_=before[:], compare_op=ALU.is_gt, fill=0.0, base=0,
                               pattern=[[1, P]], channel_multiplier=-1).then_inc(pool_const, 1)
            pool.iota(rank8[:], [[0, TILES], [-1, EXPERTS]], base=EXPERTS, channel_multiplier=0,
                      allow_small_or_imprecise_dtypes=True).then_inc(pool_const, 1)
            pool.iota(steps[:], [[0, EXPERTS], [P, TILES]], base=0, channel_multiplier=0,
                      allow_small_or_imprecise_dtypes=True).then_inc(pool_const, 1)
            pool.iota(tile_no[:], [[1, XT], [0, EXPERTS - 1]], base=0, channel_multiplier=0,
                      allow_small_or_imprecise_dtypes=True).then_inc(pool_const, 1)

            norms = [0]

            def rstd_of(done, need, half):
                n = norms[0]
                norms[0] += 1
                pool.wait_ge(done, need)
                if n == 0:
                    pool.wait_ge(pool_const, 3)
                else:
                    pool.wait_ge(rstd_done, n)
                pool.tensor_scalar(veps[:], mv[:, half * BT:(half + 1) * BT, 1], EPS, None, ALU.add).then_inc(veps_done, 1)
                pool.wait_ge(veps_done, n + 1)
                pool.tensor_tensor(rstd[:, n * BT:(n + 1) * BT], veps[:], mhalf[:], ALU.pow).then_inc(rstd_done, 1)

            for b in range(BLOCKS):
                if b + 2 < BLOCKS:
                    pool.wait_ge(qT_ps, 2 * (b + 2))
                    gather(b + 2)
                rstd_of(mv_done, (b + 1) * BT, b % 2)

            def split(s, slot):
                for c in range(3):
                    o = slot * SLOT + c * WCH
                    hi = w_slots[:, o:o + WCH]
                    if s == 0:
                        pool.wait_ge(stage_land[c], 32 if c < 2 else 48)
                    else:
                        pool.wait_ge(expert_land[c], 16 * s)
                    pool.tensor_scalar(hi, stage[:, c, :], 1.0, 1.0, ALU.mult, ALU.mult).then_inc(split_hi, 1)
                    pool.wait_ge(split_hi, s * 3 + c + 1)
                    pool.tensor_tensor(w_slots[:, o + PART:o + PART + WCH], stage[:, c, :], f32(hi),
                                       ALU.subtract).then_inc(split_lo, 1)
                    pool.wait_ge(split_lo, s * 3 + c + 1)
                    load(s, c)

            def load(e, c):
                src = (ew1, ew2, ew3)[c]
                if isinstance(e, int):
                    pool.dma_start(stage[:, c, :], src[e]).then_inc(expert_land[c], 16)
                else:
                    pool.dma_start(stage[:, c, :], src[bass.ds(e, 1)].rearrange("a p n -> p (a n)")).then_inc(expert_land[c], 16)

            split(0, 0)

            def residual(b):
                for m in range(b * BT // 2, (b + 1) * BT // 2):
                    v = slice(2 * m, 2 * m + 2)
                    pool.wait_ge(state_rows, m + 1)
                    pool.tensor_tensor(res[:, v, :], xn2[:, v, :], res[:, v, :], ALU.add).then_inc(res_done, 1)

            for b in range(BLOCKS):
                residual(b)
                rstd_of(mv2_done, (b + 1) * BT, b % 2)
            pool.wait_ge(xl_ps, 1)
            split(1, 1)

            pool.wait_ge(placed, 1)
            pool.wait_ge(zeroed, 16 * XT)
            for t in range(TILES):
                pool.indirect_dma_start(
                    out=x_sorted, out_offset=bass.IndirectOffsetOnAxis(ap=pos[:, t:t + 1], axis=0),
                    in_=xn2[:, t, :], in_offset=None,
                    bounds_check=XT * P - 1, oob_is_err=True).then_inc(scattered, 16)

            pool.wait_ge(scattered, 16 * TILES)
            pool.wait_ge(x_ps, FRONT)
            for k in range(KD):
                pool.tensor_scalar(xbT[:, 0, k, :].rearrange("p (t n) -> p t n", n=P), xlT[:, FRONT:TILES, k, :], 1.0, 1.0,
                                   ALU.mult, ALU.mult).then_inc(xb_hi, 1)
            for k in range(KD):
                pool.wait_ge(xb_hi, k + 1)
                pool.tensor_tensor(xbT[:, 1, k, :].rearrange("p (t n) -> p t n", n=P), xlT[:, FRONT:TILES, k, :],
                                   f32(xbT[:, 0, k, :]).rearrange("p (t n) -> p t n", n=P), ALU.subtract).then_inc(xb_lo, 1)
            back = back_of(pool)
            with pool.Fori(2, EXPERTS) as e:
                for c in range(3):
                    pool.wait_ge(split_lo, e * 3 + (c + 1))
                    pool.sem_inc(pool_turn, 1)
                    load(e, c)
            for c, src in enumerate((w1s, w2s, w3s)):
                pool.wait_ge(split_lo, EXPERTS * 3 + c + 1)
                pool.dma_start(stage[:, c, :], src).then_inc(expert_land[c], 16)

            pool.wait_ge(split_lo, 3 * SPLITS)
            pool.wait_ge(y_stored, back * 16 - 16 * FRONT)
            pool.sem_inc(pool_turn, 1)
            for t in range(TILES):
                pool.indirect_dma_start(
                    out=fetched[:, t, :], out_offset=None, in_=y_sorted,
                    in_offset=bass.IndirectOffsetOnAxis(ap=pos[:, t:t + 1], axis=0),
                    bounds_check=XT * P - 1, oob_is_err=True).then_inc(fetch_land, 16)

        @block.tensor
        def _(pe):
            def q_transposes(b):
                if b == 0:
                    pe.wait_ge(pool_const, 2)
                elif b == 1:
                    pe.wait_ge(qT_lo, 2)
                else:
                    pe.wait_ge(x1_lo, 2 * (b - 1))
                pe.wait_ge(q_land[b], 16 * BT)
                for k in range(KD):
                    for i in range(BT):
                        last = pe.transpose(ps[:, flip_banks[k], i * P:(i + 1) * P], q[:, i, k * P:(k + 1) * P], ident[:])
                    last.then_inc(qT_ps, 1)

            def mlp_up(b):
                for h in range(HC):
                    n = b * HC + h
                    if n == 0:
                        pe.wait_ge(w1_lo, 1)
                    if n == HC // 2:
                        pe.wait_ge(w1_lo, 2)
                    if n >= len(up_banks):
                        pe.wait_ge(h_lo, n - len(up_banks) + 1)
                    for k in range(KD):
                        if h == 0:
                            pe.wait_ge(qT_lo, 2 * b + k + 1)
                        cols = slice(h * P, (h + 1) * P)
                        last = mm3(pe, ps[:, up_banks[n % len(up_banks)], :], w1p[:, 0, k, cols], w1p[:, 1, k, cols],
                                   qTp[:, 0, k, :], qTp[:, 1, k, :], k == 0, k == KD - 1)
                    last.then_inc(h_ps, 1)
                    if b and h == FLIP_AFTER:
                        x_transposes(b - 1, flip_banks)

            def x_transposes(b, banks):
                pe.wait_ge(xn_done, BT * (b + 1))
                if banks == flip_banks:
                    pe.wait_ge(qT_lo, 2 * (b + 2))
                else:
                    pe.wait_ge(rec_done, TILES)
                for k in range(KD):
                    for i in range(BT):
                        last = pe.transpose(ps[:, banks[k], i * P:(i + 1) * P], xnb[:, i, k * P:(k + 1) * P], ident[:])
                    last.then_inc(xT_ps, 1)

            def mlp_down(b):
                if b == 0:
                    pe.wait_ge(w2_lo, 1)
                for i in range(BT):
                    t = b * BT + i
                    if t >= 2:
                        pe.wait_ge(rec_done, t - 1)
                    for h in range(HC):
                        if i == 0:
                            pe.wait_ge(h_lo, HC * b + h + 1)
                        cols = slice(i * P, (i + 1) * P)
                        last = mm3(pe, ps[:, rec_banks[t % 2], 0:D], hTp[:, 0, h, cols], hTp[:, 1, h, cols],
                                   w2p[:, 0, h, :], w2p[:, 1, h, :], h == 0, h == HC - 1)
                    last.then_inc(rec_ps, 1)

            q_transposes(0)
            for b in range(BLOCKS):
                mlp_up(b)
                if b + 1 < BLOCKS:
                    q_transposes(b + 1)
                mlp_down(b)

            def gru(u):
                layer, b, hc = units[u]
                cols = slice(b * NB, (b + 1) * NB)
                if layer == 0:
                    src = lambda part, k: (x1hi, x1lo)[part][:, k, cols]
                    pe.wait_ge(x1_lo, 2 * (b + 1))
                else:
                    src = lambda part, k: h0p[:, part, k, cols]
                    pe.wait_ge(h0_lo, last_unit[0, b] + 1)
                if u == 0:
                    pe.wait_ge(gru_lo, 1)
                    pe.wait_ge(x1_lo, 2 * (BLOCKS - 1))
                if u == 2:
                    pe.wait_ge(rec_done, TILES)
                if u >= RG:
                    pe.wait_ge(scanned, u - RG + 1)
                for g, done in enumerate((k_ps, p_ps)):
                    for k in range(KD):
                        w = slice(hc * P, (hc + 1) * P)
                        last = mm3(pe, ps[:, pair(u) + g, :], gruw[:, 0, g, layer, k, w], gruw[:, 1, g, layer, k, w],
                                   src(0, k), src(1, k), k == 0, k == KD - 1)
                    last.then_inc(done, 1)
                    if u == UNITS - 1 and g == 0:
                        pe.wait_ge(state_rows, BT // 2 + 1)
                        row_transposes(0)

            def state_transposes(b):
                pe.wait_ge(scanned, last_unit[1, b] + 1)
                if b == 0:
                    pe.wait_ge(x1_lo, 2 * BLOCKS)
                if b == 2:
                    pe.wait_ge(scanned, UNITS)
                for i in range(BT):
                    t = b * BT + i
                    if b in (1, 3):
                        pe.wait_ge(state_rows, t // 2 - 1)
                    for k in range(KD):
                        last = pe.transpose(ps[:, state_banks[b][i // 2], (i % 2) * D + k * P:(i % 2) * D + (k + 1) * P],
                                            h1[:, k, t * P:(t + 1) * P], ident[:])
                    if i % 2:
                        last.then_inc(h1T_ps, 1)

            def row_transposes(i):
                peeled = isinstance(i, int) and i < PEELED
                if peeled:
                    pe.wait_ge(xn2_done, i + 1)
                else:
                    pe.wait_ge(x_land, 16 * i + 16 * (1 - PEELED))
                row = xn2[:, i, :] if peeled else x_row
                for k in range(KD):
                    last = pe.transpose(ps[:, 6, k * P:(k + 1) * P], row[:, k * P:(k + 1) * P], ident[:])
                last.then_inc(x_ps, 1)

            for u in range(len(units)):
                gru(u)
                if u == KD - 1:
                    x_transposes(BLOCKS - 1, late_banks)
                b = (u - U0) // KD - 1
                if u >= U0 and (u - U0) % KD == KD - 1 and 0 <= b < 2:
                    state_transposes(b)

            def x2_transposes(b):
                pe.wait_ge(xn2_done, (b + 1) * BT)
                if b % 2:
                    pe.wait_ge(xl_act, b)
                    pe.wait_ge(xl_dve, b)
                else:
                    pe.wait_ge(gT_lo, 2 + b)
                for i in range(BT):
                    for k in range(KD):
                        at_ = (i % 2) * D + k * P
                        last = pe.transpose(ps[:, 4 + i // 2, at_:at_ + P], xn2[:, b * BT + i, k * P:(k + 1) * P], ident[:])
                last.then_inc(xl_ps, 1)

            def router_logits(half):
                pe.wait_ge(xl_act, 2 * half + 2)
                pe.wait_ge(xl_dve, 2 * half + 2)
                for t in range(TILES // 2):
                    for k in range(KD):
                        last = pe.matmul(ps[:, 6, t * EXPERTS:(t + 1) * EXPERTS], xlT[:, half * TILES // 2 + t, k, :],
                                         wgs[:, k, :], start=(k == 0), stop=(k == KD - 1))
                last.then_inc(logit_ps, 1)

            def up_half(i, slot, n):
                for w, done in enumerate((a_ps, b_ps)):
                    for k in range(KD):
                        o = w * WCH + k * HID + n * NB
                        last = mm3(pe, ps[:, 2 * n + w, :], xTp[:, 0, k, :], xTp[:, 1, k, :],
                                   w_slots[:, bass.ds(slot + o, NB)], w_slots[:, bass.ds(slot + (o + PART), NB)],
                                   k == 0, k == KD - 1)
                    last.then_inc(done, 1)

            def up(i, slot):
                pe.wait_ge(xT_lo, i + 1)
                for n in range(NH):
                    up_half(i, slot, n)

            def down(i, slot):
                for c in range(HC):
                    if c % (HC // NH) == 0:
                        pe.wait_ge(gT_lo, 2 * i + 1 + c // (HC // NH))
                    o = 2 * WCH + c * D
                    last = mm3(pe, ps[:, 7, 0:D], gTp[:, 0, c, :], gTp[:, 1, c, :],
                               w_slots[:, bass.ds(slot + o, D)], w_slots[:, bass.ds(slot + (o + PART), D)],
                               c == 0, c == HC - 1)
                last.then_inc(tile_done, 1)

            def g_transposes(i):
                for n in range(NH):
                    pe.wait_ge(g_done, 2 * i + n + 1)
                    for c in range(HC // NH):
                        j = n * (HC // NH) + c
                        last = pe.transpose(ps[:, 4 + n, c * P:(c + 1) * P], g_buf[:, j * P:(j + 1) * P], ident[:])
                    last.then_inc(gT_ps, 1)

            pe.wait_ge(split_lo, 3)
            pe.wait_ge(small_land, 80)
            for i in range(PEELED):
                pe.wait_ge(xT_lo, i + 1)
                if i >= 2:
                    router_logits(i - 2)
                if i == 0:
                    pe.wait_ge(scanned, UNITS - 2)
                up_half(i, 0, 0)
                if i == 0:
                    state_transposes(2)
                elif i < 3:
                    x2_transposes(2 * i - 2)
                else:
                    pe.wait_ge(onehot_done, 1)
                    pe.wait_ge(pool_const, 8)
                    pe.wait_ge(dve_const, 1)
                    oh = onehot[:].rearrange("p t e -> p (t e)")
                    pe.matmul(ps[:, 6, 0:TE], before[:], oh, start=True, stop=True)
                    pe.matmul(ps[:, 6, TE:2 * TE], ones[:], oh, start=True, stop=True).then_inc(rank_ps, 1)
                up_half(i, 0, 1)
                if i == 3:
                    pe.wait_ge(router, 1)
                elif i == 2:
                    pe.wait_ge(logits_taken, 1)
                row_transposes(i + 1)
                if i == 0:
                    state_transposes(3)
                elif i < 3:
                    x2_transposes(2 * i - 1)
                if i:
                    if i >= 2:
                        pe.wait_ge(y_taken, i - 1)
                    down(i - 1, 0)
                if i == 0:
                    pe.wait_ge(state_rows, TILES // 2)
                elif i < 3:
                    pe.wait_ge(xl_act, 2 * i)
                    pe.wait_ge(xl_dve, 2 * i)
                g_transposes(i)
            with pe.Fori(PEELED, FRONT) as i:
                up(i, 0)
                row_transposes(i + 1)
                pe.wait_ge(y_taken, i - 1)
                down(i - 1, 0)
                g_transposes(i)

            def split_of(i):
                return pe.value_load(turns[0:1, bass.ds(i, 1)], min_val=0, max_val=2 * SPLITS) >> 1

            def routed_tile(i):
                here = split_of(i)
                pe.wait_ge(split_lo, here * 3 + 2)
                up(i, (here & 1) * SLOT)
                before_ = split_of(i - 1)
                row_transposes(i + 1)
                pe.wait_ge(y_taken, i - 1)
                pe.wait_ge(split_lo, before_ * 3 + 3)
                down(i - 1, (before_ & 1) * SLOT)
                g_transposes(i)

            back = back_of(pe)
            with pe.Fori(FRONT, SURE) as i:
                routed_tile(i)
            with pe.Fori(SURE, END) as i:
                with pe.If((back - i) > 0):
                    routed_tile(i)

            def back_chunk(n):
                b, h = n // HC, n % HC
                if n == 2:
                    pe.wait_ge(gT_lo, back * 2)
                if n >= BACK_PAIRS:
                    pe.wait_ge(gb_lo, n - BACK_PAIRS + 1)
                for w, done in enumerate((ab_ps, bb_ps)):
                    for k in range(KD):
                        o = SLOT + w * WCH + k * HID + h * P
                        cols = slice(b * NB, (b + 1) * NB)
                        last = mm3(pe, ps[:, 2 * (n % BACK_PAIRS) + w, :], w_slots[:, o:o + P], w_slots[:, o + PART:o + PART + P],
                                   xbT[:, 0, k, cols], xbT[:, 1, k, cols], k == 0, k == KD - 1)
                    last.then_inc(done, 1)

            def back_rows(m):
                b, i = m // BT, m % BT
                if m == 0:
                    pe.wait_ge(xT_lo, back + 1)
                elif m == 1:
                    pe.wait_ge(y_taken, back)
                elif m < BT + 2:
                    pe.wait_ge(rows_taken, m - 1)
                else:
                    pe.wait_ge(summed, BLOCKS - 1 + m - 1 - BT)
                for h in range(HC):
                    if i == 0:
                        pe.wait_ge(gb_lo, b * HC + h + 1)
                    o = SLOT + 2 * WCH + h * D
                    cols = slice(i * P, (i + 1) * P)
                    last = mm3(pe, ps[:, 6 + m % 2, 0:D], gb(0, b, h, cols), gb(1, b, h, cols),
                               w_slots[:, o:o + D], w_slots[:, o + PART:o + PART + D], h == 0, h == HC - 1)
                last.then_inc(rows_ps, 1)

            pe.wait_ge(split_lo, 3 * SPLITS - 1)
            pe.wait_ge(xb_lo, KD)
            for n in range(CHUNKS):
                back_chunk(n)
                if n == 1:
                    pe.wait_ge(y_taken, back - 1)
                    pe.wait_ge(split_lo, 3 * SPLITS)
                    down(back - 1, EXPERTS % 2 * SLOT)
                if rows_behind(n) is not None:
                    back_rows(rows_behind(n))
            for m in range(BT, 2 * BT):
                back_rows(m)

        @block.scalar
        def _(act):
            w1v = stage[:, 0, :].rearrange("p (k n) -> p k n", k=KD)
            act.preload_act_table(ACT.Gelu_apprx_tanh)
            act.wait_ge(stage_land[0], 16)
            for h in range(2):
                cols = slice(h * NB, (h + 1) * NB)
                act.activation(w1p[:, 0, :, cols], w1v[:, :, cols], ACT.Copy).then_inc(w1_hi, 1)

            def q_hi(b):
                for k in range(KD):
                    act.wait_ge(qT_ps, 2 * b + k + 1)
                    act.activation(qTp[:, 0, k, :], ps[:, flip_banks[k], :], ACT.Copy).then_inc(qT_hi, 1)

            def x_hi(b, banks):
                for k in range(KD):
                    act.wait_ge(xT_ps, 2 * b + k + 1)
                    act.activation(x1hi[:, k, b * NB:(b + 1) * NB], ps[:, banks[k], :], ACT.Copy).then_inc(x1_hi, 1)

            q_hi(0)
            act.wait_ge(small_land, 80)
            for b in range(BLOCKS):
                for h in range(HC):
                    n = b * HC + h
                    act.wait_ge(h_ps, n + 1)
                    act.activation(ps[:, up_banks[n % len(up_banks)], :], ps[:, up_banks[n % len(up_banks)], :], ACT.Gelu_apprx_tanh,
                                   bias=b1[:, h:h + 1]).then_inc(h_gelu, 1)
                    act.wait_ge(h_gelu, n + 1)
                    act.activation(hTp[:, 0, h, :], ps[:, up_banks[n % len(up_banks)], :], ACT.Copy).then_inc(h_hi, 1)
                    if b and h == FLIP_AFTER:
                        x_hi(b - 1, flip_banks)
                if b + 1 < BLOCKS:
                    q_hi(b + 1)

            def state_hi(u):
                _, b, hc = units[u]
                act.wait_ge(scanned, u + 1)
                act.activation(h0p[:, 0, hc, b * NB:(b + 1) * NB], h_full[:, u % HF, :], ACT.Copy).then_inc(h0_hi, 1)

            def row_hi(i):
                act.wait_ge(x_ps, i + 1)
                act.activation(xTp[:, 0, :, :].rearrange("p k n -> p (k n)"), ps[:, 6, 0:D], ACT.Copy).then_inc(xT_hi, 1)

            def state_out(b):
                for m in range(BT // 2):
                    t = b * BT + 2 * m
                    act.wait_ge(h1T_ps, t // 2 + 1)
                    act.activation(xn2[:, t:t + 2, :].rearrange("p t d -> p (t d)"), ps[:, state_banks[b][m], :],
                                   ACT.Copy).then_inc(state_rows, 1)

            act.preload_act_table(ACT.Sigmoid)
            act.wait_ge(dve_const, 1)
            for u, (layer, b, hc) in enumerate(units):
                c = layer * KD + hc
                bank = pair(u)
                if u >= U0 + 2 * KD and (u - U0) % KD == 0:
                    state_out((u - U0) // KD - 2)
                act.wait_ge(k_ps, u + 1)
                act.activation(a_gate[:, u % RG, :], ps[:, bank, :], ACT.Sigmoid, bias=nbz[:, c:c + 1],
                               scale=-1.0).then_inc(gates, 1)
                act.activation(ps[:, bank, :], ps[:, bank, :], ACT.Sigmoid, bias=bz[:, c:c + 1]).then_inc(gates, 1)
                if u == UNITS - 1:
                    row_hi(0)
                act.wait_ge(p_ps, u + 1)
                act.activation(v_gate[:, u % RG, :], ps[:, bank + 1, :], ACT.Sigmoid,
                               bias=bh[:, c:c + 1]).then_inc(gates, 1)
                if 1 <= u <= U0:
                    state_hi(u - 1)
                if u == KD - 1:
                    x_hi(BLOCKS - 1, late_banks)

            act.preload_act_table(ACT.Gelu)

            def x2T(b):
                act.wait_ge(xl_ps, b + 1)
                act.activation(xlT[:, b * BT:b * BT + 2, :, :].rearrange("p t k n -> p (t k n)"), ps[:, 4, :],
                               ACT.Copy).then_inc(xl_act, 1)

            def tile(i, between=lambda c: None):
                for n in range(NH):
                    act.wait_ge(a_ps, 2 * i + n + 1)
                    act.activation(gelu_buf[:, n, :], ps[:, 2 * n, :], ACT.Gelu).then_inc(gelu_done, 1)
                    if n == 0:
                        between(0)
                row_hi(i + 1)
                between(1)
                for n in range(NH):
                    act.wait_ge(gT_ps, 2 * i + n + 1)
                    act.activation(gTp[:, 0, n * BT:(n + 1) * BT, :].rearrange("p c n -> p (c n)"), ps[:, 4 + n, :],
                                   ACT.Copy).then_inc(gT_hi, 1)
                between(2)

            tile(0, lambda c: state_out(c + 2) if c < 2 else None)
            for i in (1, 2):
                tile(i, lambda c: x2T(2 * i - 2 + c) if c < 2 else None)
            with act.Fori(PEELED - 1, FRONT) as i:
                tile(i)
            act.wait_ge(routed, 1)
            def routed_tile(i):
                turn = act.value_load(turns[0:1, bass.ds(i, 1)], min_val=0, max_val=2 * SPLITS)
                s = turn >> 1

                def next_hi(c):
                    with act.If((turn & 1) > 0):
                        act.wait_ge(expert_land[c], s * 16 + 16)
                        act.sem_inc(act_turn, 1)
                        act.activation(w_slots[:, bass.ds(((s + 1) & 1) * SLOT + c * WCH, WCH)], stage[:, c, :],
                                       ACT.Copy).then_inc(split_hi, 1)

                tile(i, next_hi)

            with act.Fori(FRONT, SURE) as i:
                routed_tile(i)
            back = back_of(act)
            with act.Fori(SURE, END) as i:
                with act.If((back - i) > 0):
                    routed_tile(i)
            act.wait_ge(split_lo, 3 * SPLITS)
            for n in range(CHUNKS):
                a_bank, b_bank = 2 * (n % BACK_PAIRS), 2 * (n % BACK_PAIRS) + 1
                act.wait_ge(ab_ps, n + 1)
                act.activation(gelub[:, n % 2, :], ps[:, a_bank, :], ACT.Gelu).then_inc(gelub_done, 1)
                act.wait_ge(gb_done, n + 1)
                act.activation(gb(0, n // HC, n % HC, slice(0, NB)), ps[:, b_bank, :], ACT.Copy).then_inc(gb_hi, 1)

        @block.vector
        def _(dve):
            w1v = stage[:, 0, :].rearrange("p (k n) -> p k n", k=KD)
            for h in range(2):
                cols = slice(h * NB, (h + 1) * NB)
                dve.wait_ge(w1_hi, h + 1)
                dve.tensor_tensor(w1p[:, 1, :, cols], w1v[:, :, cols], f32(w1p[:, 0, :, cols]), ALU.subtract).then_inc(w1_lo, 1)

            def q_lo(b):
                for k in range(KD):
                    dve.wait_ge(qT_hi, 2 * b + k + 1)
                    dve.tensor_tensor(qTp[:, 1, k, :], ps[:, flip_banks[k], :], f32(qTp[:, 0, k, :]), ALU.subtract).then_inc(qT_lo, 1)

            def x_lo(b, banks):
                for k in range(KD):
                    cols = slice(b * NB, (b + 1) * NB)
                    dve.wait_ge(x1_hi, 2 * b + k + 1)
                    dve.tensor_tensor(x1lo[:, k, cols], ps[:, banks[k], :], f32(x1hi[:, k, cols]), ALU.subtract).then_inc(x1_lo, 1)

            def moments(source, n, half, waited, bn, mvs):
                i = n % BT
                dve.wait_ge(waited, n + 1)
                dve.bn_stats(stats[:, i, :], source).then_inc(bn, 1)
                dve.wait_ge(bn, n + 1)
                dve.bn_aggr(mv[:, half * BT + i, :], stats[:, i, :]).then_inc(mvs, 1)

            def normed(dst, source, n, half, i, done):
                m = half * BT + i
                return dve.tensor_scalar(dst, source, mv[:, m, 0:1], rstd[:, n * BT + i:n * BT + i + 1],
                                         ALU.subtract, ALU.mult).then_inc(done, 1)

            def x_norm(b, i):
                if i == 0:
                    dve.wait_ge(rstd_done, b + 1)
                    if b:
                        dve.wait_ge(xT_ps, 2 * b)
                normed(xnb[:, i, :], res[:, b * BT + i, :], b, b % 2, i, xn_done)

            q_lo(0)
            dve.wait_ge(small_land, 80)
            for b in range(BLOCKS):
                for h in range(HC):
                    n = b * HC + h
                    if b and h < BT:
                        x_norm(b - 1, h)
                    dve.wait_ge(h_hi, n + 1)
                    dve.tensor_tensor(hTp[:, 1, h, :], ps[:, up_banks[n % len(up_banks)], :], f32(hTp[:, 0, h, :]), ALU.subtract).then_inc(h_lo, 1)
                    if b and h == FLIP_AFTER:
                        x_lo(b - 1, flip_banks)
                if b + 1 < BLOCKS:
                    q_lo(b + 1)
                if b == 0:
                    dve.memset(ones[:], 1.0)
                    dve.tensor_scalar(nbz[:], bz[:], -1.0, None, ALU.mult)
                    dve.tensor_scalar(bh5[:], bh[:], 0.5, None, ALU.add).then_inc(dve_const, 1)
                for i in range(BT):
                    t = b * BT + i
                    dve.wait_ge(rec_ps, t + 1)
                    dve.tensor_tensor(res[:, t, :], ps[:, rec_banks[t % 2], 0:D], b2r[:], ALU.add).then_inc(rec_done, 1)
                    moments(res[:, t, :], t, b % 2, rec_done, bn_done, mv_done)

            for i in range(BT):
                x_norm(BLOCKS - 1, i)

            def x2_norm(b, tiles=range(BT)):
                dve.wait_ge(rstd_done, BLOCKS + b + 1)
                for i in tiles:
                    normed(xn2[:, b * BT + i, :], res[:, b * BT + i, :], BLOCKS + b, b % 2, i, xn2_done)

            def x2_moments(b):
                for i in range(BT):
                    n = b * BT + i
                    dve.wait_ge(res_done, n // 2 + 1)
                    dve.bn_stats(stats[:, i, :], res[:, n, :]).then_inc(bn2_done, 1)
                for i in range(BT):
                    n = b * BT + i
                    dve.wait_ge(bn2_done, n + 1)
                    dve.bn_aggr(mv[:, b % 2 * BT + i, :], stats[:, i, :]).then_inc(mv2_done, 1)

            def state_lo(u):
                _, b, hc = units[u]
                cols = slice(b * NB, (b + 1) * NB)
                dve.wait_ge(h0_hi, u + 1)
                dve.tensor_tensor(h0p[:, 1, hc, cols], h_full[:, u % HF, :], f32(h0p[:, 0, hc, cols]),
                                  ALU.subtract).then_inc(h0_lo, 1)

            def row_lo(i):
                dve.wait_ge(xT_hi, i + 1)
                dve.tensor_tensor(xTp[:, 1, :, :].rearrange("p k n -> p (k n)"), ps[:, 6, 0:D],
                                  f32(xTp[:, 0, :, :].rearrange("p k n -> p (k n)")), ALU.subtract).then_inc(xT_lo, 1)

            carries = 0
            dve.wait_ge(dve_const, 1)
            for u, (layer, b, hc) in enumerate(units):
                c = layer * KD + hc
                bank = pair(u)
                g = v_gate[:, u % RG, :]
                if u == UNITS - 4:
                    x2_moments(0)
                if u == UNITS - 3:
                    x2_norm(0, [0])
                if u == UNITS - 1:
                    row_lo(0)
                dve.wait_ge(gates, 3 * u + 3)
                dve.scalar_tensor_tensor(out=g, in0=ps[:, bank + 1, :], scalar=bh5[:, c:c + 1], in1=g, op0=ALU.add,
                                         op1=ALU.max).then_inc(gate_steps, 1)
                dve.wait_ge(gate_steps, 2 * u + 1)
                dve.tensor_tensor(g, ps[:, bank, :], g, ALU.mult).then_inc(gate_steps, 1)
                if u == KD - 1:
                    x_lo(BLOCKS - 1, late_banks)
                dve.wait_ge(gate_steps, 2 * u + 2)
                first_block = b % SB == 0
                if layer == 0:
                    if u >= HF:
                        dve.wait_ge(h0_lo, u - HF + 1)
                    h = h_full[:, u % HF, :]
                    m = (b // SB) * KD + hc
                    init = H0 if first_block else carry[:, m:m + 1]
                    if not first_block:
                        dve.wait_ge(carried, carries)
                else:
                    h = h1[:, hc, b * NB:(b + 1) * NB]
                    init = H0 if first_block else h1[:, hc, b * NB - 1:b * NB]
                    if not first_block:
                        dve.wait_ge(scanned, last_unit[1, b - 1] + 1)
                dve.tensor_tensor_scan(h, a_gate[:, u % RG, :], g, init, ALU.mult, ALU.add).then_inc(scanned, 1)
                if layer == 0 and first_block:
                    dve.wait_ge(scanned, u + 1)
                    dve.tensor_copy(carry[:, m:m + 1], h[:, NB - 1:NB]).then_inc(carried, 1)
                    carries += 1
                if 1 <= u <= U0:
                    state_lo(u - 1)

            def x2T(b):
                dve.wait_ge(xl_ps, b + 1)
                dve.tensor_copy(xlT[:, b * BT + 2:(b + 1) * BT, :, :].rearrange("p t k n -> p (t k n)"), ps[:, 5, :]).then_inc(xl_dve, 1)

            steps_done = [0]

            def step(ins):
                steps_done[0] += 1
                ins.then_inc(router, 1)
                dve.wait_ge(router, steps_done[0])

            def over_experts(ap):
                return ap.unsqueeze(2).to_broadcast([P, TILES, EXPERTS])

            chosen = [0]

            def choose(ins):
                chosen[0] += 1
                ins.then_inc(onehot_steps, 1)
                dve.wait_ge(onehot_steps, chosen[0])

            def take_logits(half):
                v = slice(half * TILES // 2, (half + 1) * TILES // 2)
                dve.wait_ge(logit_ps, half + 1)
                dve.tensor_copy(logits[:, v, :].rearrange("p t e -> p (t e)"), ps[:, 6, 0:TE // 2]).then_inc(logits_taken, 1)

            def choose_experts():
                dve.wait_ge(pool_const, 8)
                dve.wait_ge(logits_taken, 2)
                choose(dve.tensor_reduce(best[:], logits[:], AX, ALU.max))
                choose(dve.tensor_tensor(score[:], logits[:], over_experts(best[:]), ALU.is_ge))
                choose(dve.tensor_tensor(score[:], score[:], rank8[:], ALU.mult))
                choose(dve.tensor_reduce(first[:], score[:], AX, ALU.max))
                dve.tensor_tensor(onehot[:], rank8[:], over_experts(first[:]), ALU.is_equal).then_inc(onehot_done, 1)

            def gated_half(i, n):
                dve.wait_ge(gelu_done, 2 * i + n + 1)
                dve.wait_ge(b_ps, 2 * i + n + 1)
                dve.tensor_tensor(g_buf[:, n * NB:(n + 1) * NB], ps[:, 2 * n + 1, :], gelu_buf[:, n, :],
                                  ALU.mult).then_inc(g_done, 1)

            def gated(i):
                for n in range(NH):
                    gated_half(i, n)

            def gated_lo(i):
                for n in range(NH):
                    half = slice(n * BT, (n + 1) * BT)
                    dve.wait_ge(gT_hi, 2 * i + n + 1)
                    dve.tensor_tensor(gTp[:, 1, half, :].rearrange("p c n -> p (c n)"), ps[:, 4 + n, :],
                                      f32(gTp[:, 0, half, :].rearrange("p c n -> p (c n)")), ALU.subtract).then_inc(gT_lo, 1)

            def add_shared(i, t):
                r = res[:, bass.ds(t, 1), :].rearrange("p a d -> p (a d)")
                dve.wait_ge(tile_done, i + 1)
                dve.tensor_tensor(r, ps[:, 7, 0:D], r, ALU.add).then_inc(y_taken, 1)

            x2_norm(0, range(1, BT))
            x2_moments(1)
            for i in range(PEELED):
                if i >= 2:
                    take_logits(i - 2)
                if i == 3:
                    choose_experts()
                gated_half(i, 0)
                if i == 0:
                    x2_norm(1)
                elif i < 3:
                    x2T(2 * i - 2)
                else:
                    dve.wait_ge(rank_ps, 1)
                    dve.tensor_copy(ranks[:].rearrange("p a n -> p (a n)"), ps[:, 6, 0:2 * TE]).then_inc(router, 1)
                    steps_done[0] = 1
                gated_half(i, 1)
                row_lo(i + 1)
                if i == 0:
                    x2_moments(2)
                elif i < 3:
                    x2T(2 * i - 1)
                if i == 1:
                    x2_moments(3)
                if i:
                    add_shared(i - 1, i - 1)
                gated_lo(i)
                if i == 0:
                    x2_norm(2)
                elif i == 1:
                    x2_norm(3)

            dve.wait_ge(router, 1)
            step(dve.tensor_copy(totals[:], ranks[:, 1, :].rearrange("p (t e) -> p e t", e=EXPERTS)))
            flat = totals[:].rearrange("p e t -> p (e t)")
            step(dve.tensor_tensor_scan(upto[:], ones[:, 0:TE], flat, 0.0, ALU.mult, ALU.add))
            step(dve.tensor_tensor(upto[:], upto[:], flat, ALU.subtract))
            step(dve.tensor_reduce(counts[:], totals[:], AX, ALU.add))
            step(dve.memset(steps[:, :, 0:1], -1.0))
            step(dve.tensor_tensor(over[:], counts[:].unsqueeze(2).to_broadcast([P, EXPERTS, TILES]), steps[:], ALU.is_gt))
            step(dve.tensor_reduce(tiles_e[:], over[:], AX, ALU.add))
            step(dve.tensor_tensor_scan(tiles_upto[:], ones[:, 0:EXPERTS], tiles_e[:], 0.0, ALU.mult, ALU.add))
            step(dve.tensor_tensor(first_row[:], tiles_upto[:], tiles_e[:], ALU.subtract))
            upto_v = upto[:].rearrange("p (e t) -> p e t", e=EXPERTS)
            step(dve.scalar_tensor_tensor(out=shift[:], in0=first_row[:], scalar=float(P), in1=upto_v[:, :, 0],
                                          op0=ALU.mult, op1=ALU.subtract))
            step(dve.tensor_tensor(base[:], upto_v, shift[:].unsqueeze(2).to_broadcast([P, EXPERTS, TILES]), ALU.add))
            step(dve.tensor_tensor(place_te[:], ranks[:, 0, :].rearrange("p (t e) -> p t e", e=EXPERTS),
                                   base[:].rearrange("p e t -> p t e"), ALU.add))
            step(dve.tensor_tensor(place_te[:], place_te[:], onehot[:], ALU.mult))
            step(dve.tensor_reduce(pos_f[:], place_te[:], AX, ALU.add))
            dve.tensor_copy(pos[:], pos_f[:]).then_inc(placed, 1)
            upto_b = tiles_upto[:, 0:EXPERTS - 1].unsqueeze(1).to_broadcast([P, XT, EXPERTS - 1])
            step(dve.tensor_tensor(past[:], tile_no[:], upto_b, ALU.is_ge))
            step(dve.tensor_reduce(expert_f[:], past[:], AX, ALU.add))
            step(dve.memset(fresh[:, 0:1], 1.0))
            step(dve.tensor_tensor(fresh[:, 1:XT], expert_f[:, 1:XT], expert_f[:, 0:XT - 1], ALU.subtract))
            step(dve.tensor_scalar(expert_f[:], expert_f[:], 2.0, 2.0, ALU.mult, ALU.add))
            step(dve.memset(turns[:, 0:FRONT], 0))
            step(dve.tensor_tensor(turns[:, FRONT:END], expert_f[:], fresh[:], ALU.add))
            step(dve.tensor_scalar(turns[:, END:END + 1], tiles_upto[:, EXPERTS - 1:EXPERTS], -float(TILES), None, ALU.add))
            dve.memset(stats[:, 0, 0:1], 0.0).then_inc(routed, 1)

            with dve.Fori(PEELED, FRONT) as i:
                gated(i)
                row_lo(i + 1)
                add_shared(i - 1, i - 1)
                gated_lo(i)

            def routed_tile(i, take_before):
                turn = dve.value_load(turns[0:1, bass.ds(i, 1)], min_val=0, max_val=2 * SPLITS)
                s = turn >> 1

                def next_lo(c):
                    with dve.If((turn & 1) > 0):
                        to = ((s + 1) & 1) * SLOT
                        dve.wait_ge(split_hi, s * 3 + (c + 4))
                        dve.tensor_tensor(w_slots[:, bass.ds(to + (PART + c * WCH), WCH)], stage[:, c, :],
                                          f32(w_slots[:, bass.ds(to + c * WCH, WCH)]), ALU.subtract).then_inc(split_lo, 1)

                gated_half(i, 0)
                next_lo(0)
                gated_half(i, 1)
                row_lo(i + 1)
                next_lo(1)
                take_before()
                gated_lo(i)
                next_lo(2)

            def take_routed(i, stored=None):
                dve.wait_ge(tile_done, i + 1)
                if stored is not None:
                    dve.wait_ge(y_stored, stored)
                dve.tensor_copy(y_row[:], ps[:, 7, 0:D]).then_inc(y_taken, 1)

            dve.wait_ge(routed, 1)
            routed_tile(FRONT, lambda: add_shared(FRONT - 1, FRONT - 1))
            routed_tile(FRONT + 1, lambda: take_routed(FRONT))
            with dve.Fori(FRONT + 2, SURE) as i:
                routed_tile(i, lambda: take_routed(i - 1, 16 * i - 16 * (FRONT + 1)))
            back = back_of(dve)
            with dve.Fori(SURE, END) as i:
                with dve.If((back - i) > 0):
                    routed_tile(i, lambda: take_routed(i - 1, 16 * i - 16 * (FRONT + 1)))
            def back_gated(n):
                b_bank = 2 * (n % BACK_PAIRS) + 1
                dve.wait_ge(gelub_done, n + 1)
                dve.wait_ge(bb_ps, n + 1)
                dve.tensor_tensor(ps[:, b_bank, :], ps[:, b_bank, :], gelub[:, n % 2, :], ALU.mult).then_inc(gb_done, 1)
                dve.wait_ge(gb_hi, n + 1)
                dve.tensor_tensor(gb(1, n // HC, n % HC, slice(0, NB)), ps[:, b_bank, :],
                                  f32(gb(0, n // HC, n % HC, slice(0, NB))), ALU.subtract).then_inc(gb_lo, 1)

            def add_rows(m):
                dve.wait_ge(rows_ps, m + 1)
                dve.tensor_tensor(res[:, FRONT + m, :], ps[:, 6 + m % 2, 0:D], res[:, FRONT + m, :], ALU.add).then_inc(rows_taken, 1)

            def finish(n):
                v = finishes[n]
                dve.wait_ge(fetch_land, 16 * TILES)
                if v.stop > FRONT:
                    dve.wait_ge(rows_taken, v.stop - FRONT)
                dve.tensor_tensor(fetched[:, v, :], fetched[:, v, :], res[:, v, :], ALU.add).then_inc(summed, 1)

            for n in range(CHUNKS):
                back_gated(n)
                if n == 1:
                    take_routed(back - 1, back * 16 - 16 * (FRONT + 1))
                if rows_behind(n) is not None:
                    add_rows(rows_behind(n))
                if n in (HC + 4, HC + 6):
                    finish((n - HC - 4) // 2)
            finish(2)
            v = slice(TILES - BT, TILES)
            dve.tensor_tensor(fetched[:, v, :], fetched[:, v, :], res[:, v, :], ALU.add).then_inc(presummed, 1)
            dve.wait_ge(presummed, 1)
            for m in range(BT, 2 * BT):
                t = FRONT + m
                dve.wait_ge(rows_ps, m + 1)
                dve.tensor_tensor(fetched[:, t, :], ps[:, 6 + m % 2, 0:D], fetched[:, t, :], ALU.add).then_inc(summed, 1)


def kernel(x, L0_tok_codebook, L0_tok_W1, L0_tok_b1, L0_tok_W2, L0_tok_b2, L0_attn_Wz, L0_attn_bz, L0_attn_Wh,
           L0_attn_bh, L0_ffn_w1s, L0_ffn_w2s, L0_ffn_w3s, L0_ffn_W1, L0_ffn_W2, L0_ffn_W3, L0_ffn_Wg):
    import numpy as np
    import concourse.bacc as bacc
    from concourse import mybir as mb
    from concourse.bass_utils import run_bass_kernel_spmd

    def rows(a):
        a = np.asarray(a)
        k, n = a.shape[-2:]
        a = a.reshape(*a.shape[:-2], k // P, P, n)
        return np.swapaxes(a, -3, -2)

    def flat(a):
        a = rows(a)
        return a.reshape(*a.shape[:-2], -1)

    def column(a):
        return np.asarray(a).reshape(-1, P).T

    def gru(a):
        return rows(np.swapaxes(np.asarray(a), 1, 2)).transpose(1, 0, 2, 3)

    x = np.asarray(x)
    data = {
        "idx": x.reshape(-1, P).T,
        "codebook": np.asarray(L0_tok_codebook),
        "tok_w1": rows(L0_tok_W1), "tok_b1": column(L0_tok_b1),
        "tok_w2": rows(L0_tok_W2), "tok_b2": np.asarray(L0_tok_b2).reshape(1, -1),
        "gru_wz": gru(L0_attn_Wz), "gru_bz": column(L0_attn_bz),
        "gru_wh": gru(L0_attn_Wh), "gru_bh": column(L0_attn_bh),
        "w1s": flat(L0_ffn_w1s), "w2s": flat(L0_ffn_w2s), "w3s": flat(L0_ffn_w3s),
        "ew1": flat(L0_ffn_W1), "ew2": flat(L0_ffn_W2), "ew3": flat(L0_ffn_W3),
        "wg": rows(L0_ffn_Wg),
    }
    nc = bacc.Bacc("TRN2", target_bir_lowering=False, num_devices=1)
    arrays, args = {}, {}
    for name, a in data.items():
        a = np.ascontiguousarray(a)
        arrays[name + "_in"] = a
        args[name] = nc.dram_tensor(name + "_in", a.shape, mb.dt.from_np(a.dtype), kind="ExternalInput").ap()
    d = data["codebook"].shape[1]
    args["out"] = nc.dram_tensor("out_rows", (x.size, d), mb.dt.float32, kind="ExternalOutput").ap()
    build(nc, **args)
    r = run_bass_kernel_spmd(nc, [arrays], core_ids=[0])
    return r.results[0]["out_rows"].reshape(*x.shape, d)
```
